# Optimizing a Trainium2 kernel written in Bass

```python
import numpy as np
import jax
import jax.numpy as jnp

def _softmax(x, axis=-1):
    return jax.nn.softmax(x, axis=axis)

def _gelu(x):
    return jax.nn.gelu(x, approximate=True)

def _silu(x):
    return jax.nn.silu(x)

def _sigmoid(x):
    return jax.nn.sigmoid(x)

def _layernorm(x, axis=-1, eps=1e-05):
    m = jnp.mean(x, axis=axis, keepdims=True)
    v = jnp.var(x, axis=axis, keepdims=True)
    return (x - m) / jnp.sqrt(v + eps)

def _scatter_add(tgt, idx, src, axis=0):
    return tgt.at[idx].add(src)

def _segment_sum(src, seg, n):
    return jax.ops.segment_sum(src, seg, n)
kernel_name = 'mk_flamingo_gated_d4_seqx_r4_90c3b2'

def setup_inputs(seed: int=0):
    np.random.seed(seed)
    _w = jnp.asarray

    def _rec_inputs():
        import jax
        import jax.numpy as jnp
        _rk = jax.random.key(seed)
        x = -0.0002928 + 1 * jax.random.normal(jax.random.fold_in(_rk, 1), (64, 128, 256), jnp.float32)
        _lenS = 128 - jax.random.randint(jax.random.fold_in(_rk, 7), (64,), 0, max(1, 128 // 4) + 1, jnp.int32)
        _lenS2 = 128 - jax.random.randint(jax.random.fold_in(_rk, 8), (64,), 0, max(1, 128 // 4) + 1, jnp.int32)
        _ctx_1024P = jax.random.normal(jax.random.fold_in(_rk, 11), (64, 16, 256), jnp.float32)
        _ctx_1024c = jax.random.dirichlet(jax.random.fold_in(_rk, 511), 0.3 * jnp.ones((16,), jnp.float32), (64, 128))
        _ctx_1024t = jnp.einsum('bsk,bkd->bsd', _ctx_1024c, _ctx_1024P)
        _ctx_1024t = _ctx_1024t * jax.lax.rsqrt(jnp.mean(jnp.square(_ctx_1024t)) + 1e-12) * 0.953939
        ctx_1024 = -1.39393e-06 + 0.999914 * (_ctx_1024t + 0.3 * jax.random.normal(jax.random.fold_in(_rk, 611), (64, 128, 256), jnp.float32))
        _validS = jnp.arange(128)[None, :] < _lenS[:, None]
        _validS2 = jnp.arange(128)[None, :] < _lenS2[:, None]
        _causal = jnp.tril(jnp.ones((128, 128), dtype=bool))
        mask_BxS2_ff1 = jnp.where(jnp.ones((64, 128), dtype=bool), 1.0, 0.0).astype(jnp.float32)
        mask_SxS2_if1 = jnp.where(jnp.ones((128, 128), dtype=bool), 1, 0).astype(jnp.int32)
        _g = jax.random.normal(jax.random.fold_in(_rk, 9001), (2, 4), jnp.float32)
        _g = jnp.sign(_g) * jnp.maximum(jnp.abs(_g), 1.0) + (_g == 0) * 1.0
        g_xattn = _g[0]
        g_ffn = _g[1]
        return (x, ctx_1024, mask_BxS2_ff1, mask_SxS2_if1, g_xattn, g_ffn)
    x, ctx_1024, mask_BxS2_ff1, mask_SxS2_if1, g_xattn, g_ffn = _rec_inputs()

    def _L0_xattn_setup():
        import jax, jax.numpy as jnp
        import numpy as np
        B, S, D, H = (2, 512, 256, 16)
        HD = D // H
        key = jax.random.key(seed)
        ks = jax.random.split(key, 6)
        scale = 1.0 / np.sqrt(D)
        return {'x1': jax.random.normal(ks[0], (B, S, D), dtype=jnp.float32), 'x2': jax.random.normal(ks[1], (B, S, D), dtype=jnp.float32), 'x2_mask': jnp.ones((B, S), dtype=jnp.float32), 'Wq': jax.random.normal(ks[2], (D, D), dtype=jnp.float32) * scale, 'Wk': jax.random.normal(ks[3], (D, D), dtype=jnp.float32) * scale, 'Wv': jax.random.normal(ks[4], (D, D), dtype=jnp.float32) * scale, 'Wo': jax.random.normal(ks[5], (D, D), dtype=jnp.float32) * scale, 'bo': jnp.zeros((D,), dtype=jnp.float32)}
    _L0_xattn_all = _L0_xattn_setup()
    _L0_xattn_in = {k: v for k, v in _L0_xattn_all.items() if k in ('Wq', 'Wk', 'Wv', 'Wo', 'bo')}
    del _L0_xattn_all

    def _L0_ffn_setup():
        import jax, jax.numpy as jnp
        import numpy as np
        B, S, D_IN, D_OUT = (16, 1024, 256, 256)
        ACT_BITS = 8
        QB = float(2 ** (ACT_BITS - 1) - 1)
        key = jax.random.key(seed)
        k1, k2, k3 = jax.random.split(key, 3)
        x = jax.random.normal(k1, (B, S, D_IN), dtype=jnp.float32)
        ternary_weight = jax.random.randint(k2, (D_OUT, D_IN), 0, 3, dtype=jnp.int32)
        bias = jax.random.normal(k3, (D_OUT,), dtype=jnp.float32)
        act_scale = (jnp.max(jnp.abs(x)) / QB).astype(jnp.float32)
        return {'x': x, 'ternary_weight': ternary_weight, 'bias': bias, 'act_scale': act_scale}
    _L0_ffn_all = _L0_ffn_setup()
    _L0_ffn_in = {k: v for k, v in _L0_ffn_all.items() if k in ('ternary_weight', 'bias', 'act_scale')}
    del _L0_ffn_all

    def _L1_xattn_setup():
        import jax, jax.numpy as jnp
        import numpy as np
        B, N, D_MODEL, N_HEADS = (4, 512, 256, 16)
        D_K = D_MODEL // N_HEADS
        key = jax.random.key(seed)
        ks = jax.random.split(key, 7)
        s = 1.0 / np.sqrt(D_MODEL)
        return {'Q': jax.random.normal(ks[0], (B, N, D_MODEL), jnp.float32), 'K': jax.random.normal(ks[1], (B, N, D_MODEL), jnp.float32), 'V': jax.random.normal(ks[2], (B, N, D_MODEL), jnp.float32), 'w_q': jax.random.normal(ks[3], (D_MODEL, D_MODEL), jnp.float32) * s, 'w_k': jax.random.normal(ks[4], (D_MODEL, D_K), jnp.float32) * s, 'w_v': jax.random.normal(ks[5], (D_MODEL, D_K), jnp.float32) * s, 'w_o': jax.random.normal(ks[6], (D_MODEL, D_MODEL), jnp.float32) * s}
    _L1_xattn_all = _L1_xattn_setup()
    _L1_xattn_in = {k: v for k, v in _L1_xattn_all.items() if k in ('w_q', 'w_k', 'w_v', 'w_o')}
    del _L1_xattn_all

    def _L1_ffn_setup():
        import jax, jax.numpy as jnp
        import numpy as np
        BITS = 8
        LORA_RANK = 16
        LORA_ALPHA = 32
        SCALING = LORA_ALPHA / LORA_RANK

        def fake_quant_weight(w, bits=BITS):
            qmax = 2.0 ** (bits - 1) - 1
            scale = jnp.max(jnp.abs(w)) / qmax
            wq = jnp.clip(jnp.round(w / scale), -qmax - 1, qmax) * scale
            return w + jax.lax.stop_gradient(wq - w)

        def qat_lora_linear(x, W, b, A, B):
            Wq = fake_quant_weight(W)
            base = jnp.einsum('bsi,oi->bso', x, Wq) + b
            lora = jnp.einsum('bsr,or->bso', jnp.einsum('bsi,ri->bsr', x, A), B)
            return base + SCALING * lora
        key = jax.random.key(seed)
        ks = jax.random.split(key, 9)
        d, f = (256, 1024)
        s_in = 1.0 / np.sqrt(d)
        s_ff = 1.0 / np.sqrt(f)
        return {'hidden_states': jax.random.normal(ks[0], (4, 512, d), jnp.float32), 'W_fc': jax.random.normal(ks[1], (f, d), jnp.float32) * s_in, 'b_fc': jnp.zeros((f,), jnp.float32), 'A_fc': jax.random.normal(ks[2], (LORA_RANK, d), jnp.float32) * s_in, 'B_fc': jnp.zeros((f, LORA_RANK), jnp.float32), 'W_proj': jax.random.normal(ks[3], (d, f), jnp.float32) * s_ff, 'b_proj': jnp.zeros((d,), jnp.float32), 'A_proj': jax.random.normal(ks[4], (LORA_RANK, f), jnp.float32) * s_ff, 'B_proj': jnp.zeros((d, LORA_RANK), jnp.float32)}
    _L1_ffn_all = _L1_ffn_setup()
    _L1_ffn_in = {k: v for k, v in _L1_ffn_all.items() if k in ('W_fc', 'b_fc', 'A_fc', 'B_fc', 'W_proj', 'b_proj', 'A_proj', 'B_proj')}
    del _L1_ffn_all

    def _L2_xattn_setup():
        import jax, jax.numpy as jnp
        import numpy as np
        N_HEADS = 16

        def _rel_emb(table, len_q, len_k):
            P = (table.shape[0] - 1) // 2
            rel = jnp.arange(len_k)[None, :] - jnp.arange(len_q)[:, None]
            idx = jnp.clip(rel, -P, P) + P
            return table[idx]
        key = jax.random.key(seed)
        ks = jax.random.split(key, 13)
        B, S, E = (2, 512, 256)
        P = 128
        d = E // N_HEADS
        s = 0.02
        return {'q': jax.random.normal(ks[0], (B, S, E), jnp.float32), 'k': jax.random.normal(ks[1], (B, S, E), jnp.float32), 'v': jax.random.normal(ks[2], (B, S, E), jnp.float32), 'Wq': jax.random.normal(ks[3], (E, E), jnp.float32) * s, 'bq': jnp.zeros((E,), jnp.float32), 'Wk': jax.random.normal(ks[4], (E, E), jnp.float32) * s, 'bk': jnp.zeros((E,), jnp.float32), 'Wv': jax.random.normal(ks[5], (E, E), jnp.float32) * s, 'bv': jnp.zeros((E,), jnp.float32), 'Wo': jax.random.normal(ks[6], (E, E), jnp.float32) * s, 'bo': jnp.zeros((E,), jnp.float32), 'rk_table': jax.random.normal(ks[7], (2 * P + 1, d), jnp.float32) * s, 'rv_table': jax.random.normal(ks[8], (2 * P + 1, d), jnp.float32) * s}
    _L2_xattn_all = _L2_xattn_setup()
    _L2_xattn_in = {k: v for k, v in _L2_xattn_all.items() if k in ('Wq', 'bq', 'Wk', 'bk', 'Wv', 'bv', 'Wo', 'bo', 'rk_table', 'rv_table')}
    del _L2_xattn_all

    def _L2_ffn_setup():
        import jax, jax.numpy as jnp
        import numpy as np
        D_MODEL = 256
        D_OUT = 256
        RANK = 16
        NUM_TRUE = 8
        NUM_NULL = 2
        TOP_K = 2
        SCALING = 32.0 / 16.0
        key = jax.random.key(seed)
        ks = jax.random.split(key, 6)
        x = jax.random.normal(ks[0], (4, 1024, D_MODEL), dtype=jnp.float32)
        base_w = jax.random.normal(ks[1], (D_OUT, D_MODEL), dtype=jnp.float32) / np.sqrt(D_MODEL)
        base_b = jax.random.normal(ks[2], (D_OUT,), dtype=jnp.float32) * 0.01
        gate_w = jax.random.normal(ks[3], (NUM_TRUE + NUM_NULL, D_MODEL), dtype=jnp.float32) / np.sqrt(D_MODEL)
        lora_A = jax.random.normal(ks[4], (NUM_TRUE, RANK, D_MODEL), dtype=jnp.float32) / np.sqrt(D_MODEL)
        lora_B = jax.random.normal(ks[5], (NUM_TRUE, D_OUT, RANK), dtype=jnp.float32) * 0.01
        return {'x': x, 'base_w': base_w, 'base_b': base_b, 'gate_w': gate_w, 'lora_A': lora_A, 'lora_B': lora_B}
    _L2_ffn_all = _L2_ffn_setup()
    _L2_ffn_in = {k: v for k, v in _L2_ffn_all.items() if k in ('base_w', 'base_b', 'gate_w', 'lora_A', 'lora_B')}
    del _L2_ffn_all

    def _L3_xattn_setup():
        import jax, jax.numpy as jnp
        import numpy as np
        E = 256
        H = 16
        D = E // H
        key = jax.random.key(seed)
        ks = jax.random.split(key, 12)
        N, S, T = (4, 512, 512)
        inp = {'query': jax.random.normal(ks[0], (N, S, E), jnp.float32), 'key': jax.random.normal(ks[1], (N, T, E), jnp.float32), 'value': jax.random.normal(ks[2], (N, T, E), jnp.float32), 'attn_mask': jnp.ones((S, T), jnp.int32), 'Wq': jax.random.normal(ks[3], (E, E), jnp.float32) / np.sqrt(E), 'bq': jax.random.normal(ks[4], (E,), jnp.float32) * 0.01, 'Wk': jax.random.normal(ks[5], (E, E), jnp.float32) / np.sqrt(E), 'bk': jax.random.normal(ks[6], (E,), jnp.float32) * 0.01, 'Wv': jax.random.normal(ks[7], (E, E), jnp.float32) / np.sqrt(E), 'bv': jax.random.normal(ks[8], (E,), jnp.float32) * 0.01, 'Wo': jax.random.normal(ks[9], (E, E), jnp.float32) / np.sqrt(E), 'bo': jax.random.normal(ks[10], (E,), jnp.float32) * 0.01}
        return inp
    _L3_xattn_all = _L3_xattn_setup()
    _L3_xattn_in = {k: v for k, v in _L3_xattn_all.items() if k in ('Wq', 'bq', 'Wk', 'bk', 'Wv', 'bv', 'Wo', 'bo')}
    del _L3_xattn_all

    def _L3_ffn_setup():
        import jax, jax.numpy as jnp
        import numpy as np
        B, S, D, E, H, K = (64, 512, 256, 32, 1024, 8)
        key = jax.random.key(seed)
        k0, k1, k2, k3 = jax.random.split(key, 4)
        x = jax.random.normal(k0, (B, S, D), jnp.float32)
        gate_w = jax.random.normal(k1, (E, D), jnp.float32) * (1.0 / np.sqrt(D))
        gate_b = jnp.zeros((E,), jnp.float32)
        w1 = jax.random.normal(k2, (E, D + 1, H), jnp.float32) * (1.0 / np.sqrt(D + 1))
        w2 = jax.random.normal(k3, (E, H + 1, D), jnp.float32) * (1.0 / np.sqrt(H + 1))
        return {'x': x, 'gate_w': gate_w, 'gate_b': gate_b, 'w1': w1, 'w2': w2}
    _L3_ffn_all = _L3_ffn_setup()
    _L3_ffn_in = {k: v for k, v in _L3_ffn_all.items() if k in ('gate_w', 'gate_b', 'w1', 'w2')}
    del _L3_ffn_all
    return {'x': x, 'ctx_1024': ctx_1024, 'mask_BxS2_ff1': mask_BxS2_ff1, 'mask_SxS2_if1': mask_SxS2_if1, 'g_xattn': g_xattn, 'g_ffn': g_ffn, 'L0_xattn_Wq': _L0_xattn_in['Wq'], 'L0_xattn_Wk': _L0_xattn_in['Wk'], 'L0_xattn_Wv': _L0_xattn_in['Wv'], 'L0_xattn_Wo': _L0_xattn_in['Wo'], 'L0_xattn_bo': _L0_xattn_in['bo'], 'L0_ffn_ternary_weight': _L0_ffn_in['ternary_weight'], 'L0_ffn_bias': _L0_ffn_in['bias'], 'L0_ffn_act_scale': _L0_ffn_in['act_scale'], 'L1_xattn_w_q': _L1_xattn_in['w_q'], 'L1_xattn_w_k': _L1_xattn_in['w_k'], 'L1_xattn_w_v': _L1_xattn_in['w_v'], 'L1_xattn_w_o': _L1_xattn_in['w_o'], 'L1_ffn_W_fc': _L1_ffn_in['W_fc'], 'L1_ffn_b_fc': _L1_ffn_in['b_fc'], 'L1_ffn_A_fc': _L1_ffn_in['A_fc'], 'L1_ffn_B_fc': _L1_ffn_in['B_fc'], 'L1_ffn_W_proj': _L1_ffn_in['W_proj'], 'L1_ffn_b_proj': _L1_ffn_in['b_proj'], 'L1_ffn_A_proj': _L1_ffn_in['A_proj'], 'L1_ffn_B_proj': _L1_ffn_in['B_proj'], 'L2_xattn_Wq': _L2_xattn_in['Wq'], 'L2_xattn_bq': _L2_xattn_in['bq'], 'L2_xattn_Wk': _L2_xattn_in['Wk'], 'L2_xattn_bk': _L2_xattn_in['bk'], 'L2_xattn_Wv': _L2_xattn_in['Wv'], 'L2_xattn_bv': _L2_xattn_in['bv'], 'L2_xattn_Wo': _L2_xattn_in['Wo'], 'L2_xattn_bo': _L2_xattn_in['bo'], 'L2_xattn_rk_table': _L2_xattn_in['rk_table'], 'L2_xattn_rv_table': _L2_xattn_in['rv_table'], 'L2_ffn_base_w': _L2_ffn_in['base_w'], 'L2_ffn_base_b': _L2_ffn_in['base_b'], 'L2_ffn_gate_w': _L2_ffn_in['gate_w'], 'L2_ffn_lora_A': _L2_ffn_in['lora_A'], 'L2_ffn_lora_B': _L2_ffn_in['lora_B'], 'L3_xattn_Wq': _L3_xattn_in['Wq'], 'L3_xattn_bq': _L3_xattn_in['bq'], 'L3_xattn_Wk': _L3_xattn_in['Wk'], 'L3_xattn_bk': _L3_xattn_in['bk'], 'L3_xattn_Wv': _L3_xattn_in['Wv'], 'L3_xattn_bv': _L3_xattn_in['bv'], 'L3_xattn_Wo': _L3_xattn_in['Wo'], 'L3_xattn_bo': _L3_xattn_in['bo'], 'L3_ffn_gate_w': _L3_ffn_in['gate_w'], 'L3_ffn_gate_b': _L3_ffn_in['gate_b'], 'L3_ffn_w1': _L3_ffn_in['w1'], 'L3_ffn_w2': _L3_ffn_in['w2']}

def reference(x, ctx_1024, mask_BxS2_ff1, mask_SxS2_if1, g_xattn, g_ffn, L0_xattn_Wq, L0_xattn_Wk, L0_xattn_Wv, L0_xattn_Wo, L0_xattn_bo, L0_ffn_ternary_weight, L0_ffn_bias, L0_ffn_act_scale, L1_xattn_w_q, L1_xattn_w_k, L1_xattn_w_v, L1_xattn_w_o, L1_ffn_W_fc, L1_ffn_b_fc, L1_ffn_A_fc, L1_ffn_B_fc, L1_ffn_W_proj, L1_ffn_b_proj, L1_ffn_A_proj, L1_ffn_B_proj, L2_xattn_Wq, L2_xattn_bq, L2_xattn_Wk, L2_xattn_bk, L2_xattn_Wv, L2_xattn_bv, L2_xattn_Wo, L2_xattn_bo, L2_xattn_rk_table, L2_xattn_rv_table, L2_ffn_base_w, L2_ffn_base_b, L2_ffn_gate_w, L2_ffn_lora_A, L2_ffn_lora_B, L3_xattn_Wq, L3_xattn_bq, L3_xattn_Wk, L3_xattn_bk, L3_xattn_Wv, L3_xattn_bv, L3_xattn_Wo, L3_xattn_bo, L3_ffn_gate_w, L3_ffn_gate_b, L3_ffn_w1, L3_ffn_w2):
    import jax
    import jax.numpy as jnp

    def _L0_xattn_ref(x1, x2, x2_mask, Wq, Wk, Wv, Wo, bo):
        import jax, jax.numpy as jnp
        import numpy as np
        B, S, D, H = (2, 512, 256, 16)
        HD = D // H
        b, s1, d = x1.shape
        s2 = x2.shape[1]
        q = (x1 @ Wq.T).reshape(b, s1, H, HD).transpose(0, 2, 1, 3)
        k = (x2 @ Wk.T).reshape(b, s2, H, HD).transpose(0, 2, 1, 3)
        v = (x2 @ Wv.T).reshape(b, s2, H, HD).transpose(0, 2, 1, 3)
        dots = jnp.einsum('bhqd,bhkd->bhqk', q, k) / jnp.sqrt(jnp.asarray(HD, x1.dtype))
        dots = dots * x2_mask[:, None, None, :]
        causal = jnp.tril(jnp.ones((s1, s2), dtype=dots.dtype))
        dots = dots * causal
        attn = jax.nn.softmax(dots, axis=-1)
        out = jnp.einsum('bhqk,bhkd->bhqd', attn, v)
        y = out.transpose(0, 2, 1, 3).reshape(b, s1, d)
        return y @ Wo.T + bo

    def _L0_ffn_ref(x, ternary_weight, bias, act_scale):
        import jax, jax.numpy as jnp
        import numpy as np
        B, S, D_IN, D_OUT = (16, 1024, 256, 256)
        ACT_BITS = 8
        QB = float(2 ** (ACT_BITS - 1) - 1)
        scale = jnp.maximum(act_scale, 1e-05)
        x_int = jnp.clip(jnp.round(x / scale), -QB, QB)
        x_dq = jnp.nan_to_num(x_int * scale, nan=0.0, posinf=10000.0, neginf=-10000.0)
        w = ternary_weight.astype(jnp.float32) - 1.0
        return jnp.einsum('bsi,oi->bso', x_dq, w) + bias

    def _L1_xattn_ref(Q, K, V, w_q, w_k, w_v, w_o):
        import jax, jax.numpy as jnp
        import numpy as np
        B, N, D_MODEL, N_HEADS = (4, 512, 256, 16)
        D_K = D_MODEL // N_HEADS
        b, n, _ = Q.shape
        q = (Q @ w_q).reshape(b, n, N_HEADS, D_K)
        k = K @ w_k
        v = V @ w_v
        scale = 1.0 / jnp.sqrt(jnp.asarray(D_K, q.dtype))
        scores = jnp.einsum('bnhd,bmd->bhnm', q, k) * scale
        causal = jnp.triu(jnp.ones((n, n), dtype=bool), k=1)
        scores = jnp.where(causal[None, None], -jnp.inf, scores)
        weights = jax.nn.softmax(scores, axis=-1)
        attn = jnp.einsum('bhnm,bmd->bnhd', weights, v).reshape(b, n, D_MODEL)
        return attn @ w_o

    def _L1_ffn_ref(hidden_states, W_fc, b_fc, A_fc, B_fc, W_proj, b_proj, A_proj, B_proj):
        import jax, jax.numpy as jnp
        import numpy as np
        BITS = 8
        LORA_RANK = 16
        LORA_ALPHA = 32
        SCALING = LORA_ALPHA / LORA_RANK

        def fake_quant_weight(w, bits=BITS):
            qmax = 2.0 ** (bits - 1) - 1
            scale = jnp.max(jnp.abs(w)) / qmax
            wq = jnp.clip(jnp.round(w / scale), -qmax - 1, qmax) * scale
            return w + jax.lax.stop_gradient(wq - w)

        def qat_lora_linear(x, W, b, A, B):
            Wq = fake_quant_weight(W)
            base = jnp.einsum('bsi,oi->bso', x, Wq) + b
            lora = jnp.einsum('bsr,or->bso', jnp.einsum('bsi,ri->bsr', x, A), B)
            return base + SCALING * lora
        h = qat_lora_linear(hidden_states, W_fc, b_fc, A_fc, B_fc)
        h = jax.nn.gelu(h, approximate=False)
        h = qat_lora_linear(h, W_proj, b_proj, A_proj, B_proj)
        return h

    def _L2_xattn_ref(q, k, v, Wq, bq, Wk, bk, Wv, bv, Wo, bo, rk_table, rv_table):
        import jax, jax.numpy as jnp
        import numpy as np
        N_HEADS = 16

        def _rel_emb(table, len_q, len_k):
            P = (table.shape[0] - 1) // 2
            rel = jnp.arange(len_k)[None, :] - jnp.arange(len_q)[:, None]
            idx = jnp.clip(rel, -P, P) + P
            return table[idx]
        B, Sq, E = q.shape
        Sk = k.shape[1]
        H = N_HEADS
        d = E // H
        scale = jnp.sqrt(jnp.asarray(d, q.dtype))
        qh = (q @ Wq.T + bq).reshape(B, Sq, H, d).transpose(0, 2, 1, 3)
        kh = (k @ Wk.T + bk).reshape(B, Sk, H, d).transpose(0, 2, 1, 3)
        vh = (v @ Wv.T + bv).reshape(B, Sk, H, d).transpose(0, 2, 1, 3)
        qk = jnp.einsum('bhqd,bhkd->bhqk', qh, kh)
        r_k = _rel_emb(rk_table, Sq, Sk)
        q_rk = jnp.einsum('bhqd,qkd->bhqk', qh, r_k)
        attn = jax.nn.softmax((qk + q_rk) / scale, axis=-1)
        w1 = jnp.einsum('bhqk,bhkd->bhqd', attn, vh)
        r_v = _rel_emb(rv_table, Sq, Sk)
        w2 = jnp.einsum('bhqk,qkd->bhqd', attn, r_v)
        out = (w1 + w2).transpose(0, 2, 1, 3).reshape(B, Sq, E)
        return out @ Wo.T + bo

    def _L2_ffn_ref(x, base_w, base_b, gate_w, lora_A, lora_B):
        import jax, jax.numpy as jnp
        import numpy as np
        D_MODEL = 256
        D_OUT = 256
        RANK = 16
        NUM_TRUE = 8
        NUM_NULL = 2
        TOP_K = 2
        SCALING = 32.0 / 16.0
        xf = x.reshape(-1, x.shape[-1])
        logits = jnp.einsum('td,ed->te', xf, gate_w)
        probs = jax.nn.softmax(logits, axis=-1)
        weights, selected = jax.lax.top_k(probs, TOP_K)
        true_mask = (selected < NUM_TRUE).astype(weights.dtype)
        tw = weights * true_mask
        denom = tw.sum(axis=-1, keepdims=True)
        denom = jnp.where(denom > 0, denom, jnp.ones_like(denom))
        nw = tw / denom
        onehot = jax.nn.one_hot(selected, NUM_TRUE, dtype=nw.dtype)
        ew = jnp.einsum('tk,tke->te', nw, onehot)
        z = jnp.einsum('td,erd->ter', xf, lora_A)
        moe = jnp.einsum('ter,te,eor->to', z, ew, lora_B) * SCALING
        base = jnp.einsum('td,od->to', xf, base_w) + base_b
        out = (base + moe).reshape(x.shape[:-1] + (D_OUT,))
        return out

    def _L3_xattn_ref(query, key, value, attn_mask, Wq, bq, Wk, bk, Wv, bv, Wo, bo):
        import jax, jax.numpy as jnp
        import numpy as np
        E = 256
        H = 16
        D = E // H
        N, S, _ = query.shape
        T = key.shape[1]
        q = (query @ Wq.T + bq).reshape(N, S, H, D).transpose(0, 2, 1, 3)
        k = (key @ Wk.T + bk).reshape(N, T, H, D).transpose(0, 2, 1, 3)
        v = (value @ Wv.T + bv).reshape(N, T, H, D).transpose(0, 2, 1, 3)
        scores = jnp.einsum('nhsd,nhtd->nhst', q, k) / np.sqrt(D).astype(np.float32)
        scores = jnp.where(attn_mask == 0, jnp.float32(-jnp.inf), scores)
        attn = jax.nn.softmax(scores, axis=-1)
        out = jnp.einsum('nhst,nhtd->nhsd', attn, v)
        out = out.transpose(0, 2, 1, 3).reshape(N, S, E)
        return out @ Wo.T + bo

    def _L3_ffn_ref(x, gate_w, gate_b, w1, w2):
        import jax, jax.numpy as jnp
        import numpy as np
        B, S, D, E, H, K = (64, 512, 256, 32, 1024, 8)
        b, s, d = x.shape
        logits = jnp.einsum('bsd,ed->bse', x, gate_w) + gate_b
        probs = jax.nn.softmax(logits, axis=-2)
        vals_t, idx_t = jax.lax.top_k(probs.transpose(0, 2, 1), K)
        vals = vals_t.transpose(0, 2, 1)
        idx = idx_t.transpose(0, 2, 1)
        flat_idx = idx.reshape(b, K * E)
        tok = jnp.take_along_axis(x, flat_idx[:, :, None], axis=1)
        tok = tok.reshape(b, K, E, d)
        merged = jnp.einsum('bked,bke->bed', tok, vals)
        ones = jnp.ones(merged.shape[:-1] + (1,), merged.dtype)
        h = jnp.einsum('bei,eih->beh', jnp.concatenate([merged, ones], -1), w1)
        h = jax.nn.gelu(h, approximate=False)
        o = jnp.einsum('bej,ejo->beo', jnp.concatenate([h, ones], -1), w2)
        out_tok = jnp.einsum('beo,bke->bkeo', o, vals).reshape(b, K * E, d)
        out = jnp.zeros_like(x).at[jnp.arange(b)[:, None], flat_idx].add(out_tok)
        return out
    x = x + jnp.tanh(g_xattn[0]) * _L0_xattn_ref(_layernorm(x, axis=-1), ctx_1024, mask_BxS2_ff1, L0_xattn_Wq, L0_xattn_Wk, L0_xattn_Wv, L0_xattn_Wo, L0_xattn_bo)
    x = x + jnp.tanh(g_ffn[0]) * _L0_ffn_ref(_layernorm(x, axis=-1), L0_ffn_ternary_weight, L0_ffn_bias, L0_ffn_act_scale)
    x = x + jnp.tanh(g_xattn[1]) * _L1_xattn_ref(_layernorm(x, axis=-1), ctx_1024, ctx_1024, L1_xattn_w_q, L1_xattn_w_k, L1_xattn_w_v, L1_xattn_w_o)
    x = x + jnp.tanh(g_ffn[1]) * _L1_ffn_ref(_layernorm(x, axis=-1), L1_ffn_W_fc, L1_ffn_b_fc, L1_ffn_A_fc, L1_ffn_B_fc, L1_ffn_W_proj, L1_ffn_b_proj, L1_ffn_A_proj, L1_ffn_B_proj)
    x = x + jnp.tanh(g_xattn[2]) * _L2_xattn_ref(_layernorm(x, axis=-1), ctx_1024, ctx_1024, L2_xattn_Wq, L2_xattn_bq, L2_xattn_Wk, L2_xattn_bk, L2_xattn_Wv, L2_xattn_bv, L2_xattn_Wo, L2_xattn_bo, L2_xattn_rk_table, L2_xattn_rv_table)
    x = x + jnp.tanh(g_ffn[2]) * _L2_ffn_ref(_layernorm(x, axis=-1), L2_ffn_base_w, L2_ffn_base_b, L2_ffn_gate_w, L2_ffn_lora_A, L2_ffn_lora_B)
    x = x + jnp.tanh(g_xattn[3]) * _L3_xattn_ref(_layernorm(x, axis=-1), ctx_1024, ctx_1024, mask_SxS2_if1, L3_xattn_Wq, L3_xattn_bq, L3_xattn_Wk, L3_xattn_bk, L3_xattn_Wv, L3_xattn_bv, L3_xattn_Wo, L3_xattn_bo)
    x = x + jnp.tanh(g_ffn[3]) * _L3_ffn_ref(_layernorm(x, axis=-1), L3_ffn_gate_w, L3_ffn_gate_b, L3_ffn_w1, L3_ffn_w2)
    return x

_drawn_inputs = setup_inputs


def setup_inputs(seed=0):
    import zlib

    import numpy as np

    out = dict(_drawn_inputs(seed))
    spreads = {'L0_xattn_bo': (0.0, 0.1),
     'L1_ffn_b_fc': (0.0, 0.8),
     'L1_ffn_B_fc': (0.0, 0.1),
     'L1_ffn_b_proj': (0.0, 0.8),
     'L1_ffn_B_proj': (0.0, 0.1),
     'L2_xattn_bq': (0.0, 0.8),
     'L2_xattn_bk': (0.0, 2.0),
     'L2_xattn_bv': (0.0, 0.8),
     'L2_xattn_bo': (0.0, 0.8),
     'L3_ffn_gate_b': (0.0, 2.0)}
    factors = {'g_ffn': 8.0,
     'L2_xattn_Wq': 8.0,
     'L2_xattn_Wk': 8.0,
     'L2_xattn_Wv': 8.0,
     'L2_xattn_Wo': 8.0,
     'L2_xattn_rk_table': 8.0,
     'L2_xattn_rv_table': 8.0,
     'L2_ffn_base_b': 64.0,
     'L2_ffn_gate_w': 8.0,
     'L2_ffn_lora_A': 8.0,
     'L2_ffn_lora_B': 8.0,
     'L3_xattn_Wq': 3.523,
     'L3_xattn_bq': 60.445,
     'L3_xattn_Wk': 3.525,
     'L3_xattn_bk': 64.0,
     'L3_xattn_bv': 64.0,
     'L3_xattn_bo': 64.0,
     'L3_ffn_gate_w': 8.0,
     'L3_ffn_w1': 8.0,
     'L3_ffn_w2': 8.0}
    for name, (base, spread) in spreads.items():
        noise = np.random.default_rng([zlib.crc32(name.encode()), seed]).standard_normal(out[name].shape)
        drawn = base * np.exp(spread * noise) if base else spread * noise
        out[name] = jnp.asarray(drawn.astype(out[name].dtype))
    for name, factor in factors.items():
        out[name] = (out[name] * factor).astype(out[name].dtype)
    return out
```

```python
import concourse.bass as bass
from concourse import mybir
from contextlib import ExitStack
import numpy as np


STAGES = 8


def flamingo_program(nc, A, out):
    f32, bf16, i32 = mybir.dt.float32, mybir.dt.bfloat16, mybir.dt.int32
    ALU, ACT, AX = mybir.AluOpType, mybir.ActivationFunctionType, mybir.AxisListType
    RMAX = bass.bass_isa.ReduceOp.max

    NB, P, D = A["x"].shape
    H = 16
    HD = D // H
    VW = 32
    KT = D // P
    F = A["L1_ffn_W_fc"].shape[0]
    FT = F // P
    R = A["L1_ffn_A_fc"].shape[0]
    NE, _, FE = A["L3_ffn_w1"].shape
    CE = FE // P
    E2 = A["L2_ffn_lora_A"].shape[0]
    G2 = A["L2_ffn_gate_w"].shape[0]
    TOPK = 8
    GROUP = 4
    NG = NB // GROUP
    SB = 512
    BIG = float(2.0 ** 100)
    ROUND = 1.5 * 2.0 ** 23
    EPS = 1e-5
    SCALE = HD ** -0.5
    QB = 127.0
    HAS_BIAS = [0, 1, 3, 4, 5, 6]

    ctx = ExitStack()
    arena = ExitStack()

    def sb(name, shape, dt=f32, stack=ctx):
        return stack.enter_context(nc.sbuf_tensor(name, shape, dt))

    def sem(name):
        return ctx.enter_context(nc.semaphore(name))

    def wait(eng, s, value):
        if not (isinstance(value, int) and value <= 0):
            eng.wait_ge(s, value)

    def bc(ap, n, axis):
        ap = ap.unsqueeze(axis)
        shape = list(ap.shape)
        shape[axis] = n
        return ap.broadcast_to(shape)

    with ctx:
        x_all = sb("x_all", [P, NB, D])
        attn_wT = {}
        for a in range(4):
            for w in "qkvo":
                attn_wT[a, w] = sb(f"w{w}T_{a}", [P, KT, D])
        ternT = sb("ternT", [P, KT, D])
        baseT = sb("baseT", [P, KT, D])
        gateloraT = sb("gateloraT", [P, KT, G2 + P])
        lora_bT = sb("lora_bT", [P, D])
        gate3T = sb("gate3T", [P, KT, NE])
        fcT = sb("fcT", [P, KT, F])
        projT = sb("projT", [P, FT, D])
        RKW = P + HD - 1
        rkT = sb("rkT", [P, RKW])
        rv_shift = sb("rv_shift", [P, HD, P])
        ident = sb("ident", [P, P])
        ident_b = sb("ident_b", [P, P], bf16)
        causal_q = sb("causal_q", [P, P], bf16)
        later_k = sb("later_k", [P, P])
        given_q = sb("given_q", [P, P], bf16)
        row_ok = sb("row_ok", [P, 1])
        floor = sb("floor", [P, 1])
        block8 = sb("block8", [P, 8])
        block8r = sb("block8r", [P, 8])
        place16 = sb("place16", [P, 3 * HD])
        parity = sb("parity", [P, 2])
        mod16 = sb("mod16", [P, HD])
        bias_q = {a: sb(f"bias_q{a}", [P, KT]) for a in (2, 3)}
        bias_k = {a: sb(f"bias_k{a}", [P, KT]) for a in (2, 3)}
        bias_qp = sb("bias_qp", [P, KT, 2])
        bias_all = {st: sb(f"bias_{st}", [P, D]) for st in HAS_BIAS}
        gates = sb("gates", [P, 8])
        act_s = sb("act_s", [P, 4])
        b_fc = sb("b_fc", [P, FT])
        gate_b4 = sb("gate_b4", [P, 1])
        iota10 = sb("iota10", [P, G2])
        ones = sb("ones", [1, P])
        eps_t = sb("eps_t", [P, 2])
        v1 = sb("v1", [P, 2, H, VW])
        tick = sb("tick", [P, 4])
        ctx_raw = sb("ctx_raw", [P, 2, D])
        key_scale = sb("key_scale", [P, 2, P])
        mv = sb("mv", [P, 2, 2])
        bn6 = sb("bn6", [P, 2, 6])
        veps = sb("veps", [P, 2])
        rstd = sb("rstd", [P, 2])
        wide = sb("wide", [P, max(KT * NE * NB, 2 * FT * D)])
        merged = wide[:, 0:KT * NE * NB].rearrange("p (k e b) -> p k e b", k=KT, e=NE)
        quant, quant2 = wide[:, 0:FT * D], wide[:, FT * D:2 * FT * D]
        sT = projT[:, :, :].rearrange("p t n -> p (t n)")
        spread_v = fcT[:, :, :].rearrange("p k n -> p (k n)")
        qd, q2 = [wide[:, i * HD * 8 * H:(i + 1) * HD * 8 * H].rearrange("p (b a h) -> p b a h", b=HD, a=8)
                  for i in range(2)]

        ones_b = sb("ones_b", [2, P], bf16)
        query_dram = nc.dram_tensor("query_dram", (2, D, P), f32, kind="Internal").ap()
        ps = ctx.enter_context(nc.psum_tensor("ps", [P, 8, SB], f32))
        expert_out = nc.dram_tensor("expert_out", (NB, NE, D), f32, kind="Internal").ap()
        route = nc.dram_tensor("route", (NG, GROUP * NE, P), f32, kind="Internal").ap()

        def scope(*tensors):
            with ExitStack() as stack:
                return [sb(*t, stack=stack) for t in tensors]

        square = [(0, "q"), (0, "k"), (0, "v"), (0, "o"), (2, "q"), (2, "k"), (2, "v"), (2, "o"),
                  (3, "q"), (3, "k"), (3, "v"), (3, "o")]
        FREE = KT * len(square)
        raw_sq = x_all[:, NB - FREE:NB, :].rearrange("p (i m) n -> p i m n", m=KT)
        (raw_tern, raw_base, raw_gl, raw_g2, raw_lb, raw_g3, raw_fc, raw_proj, raw_bfc, raw_bproj,
         raw_afc, raw_aproj, lora_bfcT, lora_bprojT, raw_rk, raw_k1, raw_v1, bv_col, bv_rep, amax,
         raw_mask, am_f, iota_i, am_any, ternf) = scope(
            ("raw_tern", [P, KT, D], i32), ("raw_base", [P, KT, D]),
            ("raw_gl", [P, D]), ("raw_g2", [G2, D]), ("raw_lb", [P, KT, E2, R]), ("raw_g3", [NE, D]),
            ("raw_fc", [P, FT, D]), ("raw_proj", [P, KT, F]), ("raw_bfc", [P, FT, R]), ("raw_bproj", [P, KT, R]),
            ("raw_afc", [R, D]), ("raw_aproj", [R, F]), ("lora_bfcT", [R, F]), ("lora_bprojT", [R, D]),
            ("raw_rk", [P, 2, 8, HD]), ("raw_k1", [P, KT, HD]), ("raw_v1", [P, KT, HD]),
            ("bv_col", [P, 2, KT]), ("bv_rep", [P, 2, KT, P]), ("amax", [P, 12]), ("raw_mask", [P, P], i32),
            ("am_f", [P, P]), ("iota_i", [P, G2], i32), ("am_any", [P, 2]), ("ternf", [P, KT, D]))
        (xn, xcT, qm, kT, probs, on, oT, nm, nm_hl, e0, rec, mix, headT, ovT, nm_row, qu, qz, mix2, mix3) = scope(
            ("xn", [P, 2, D]), ("xcT", [P, 2, 2 * KT, P]), ("qm", [P, 2, 2, KT, P]), ("kT", [P, 2, KT, P]),
            ("probs", [P, 2, H * P]), ("on", [P, 2, D]), ("oT", [P, 2, KT, P]),
            ("nm", [P, 2, H]), ("nm_hl", [P, 1, 2, H], bf16), ("e0", [P, 2, H]),
            ("rec", [P, 2, H]), ("mix", [P, H, HD + 1]), 
            ("headT", [P, 4 * P]), ("ovT", [P, D]), ("nm_row", [2, H * P], bf16),
            ("qu", [P, 2, KT, P]), ("qz", [P, H, HD]),
            ("mix2", [P, D]), ("mix3", [P, D]))
        probsT, exps = probs[:, 0, :], probs[:, 1, :]
        (fx, fxT, fz, fzT, f_top, f_ix, f_ixf, f_e, f_s, f_w, f_r, fq) = scope(
            ("fx", [P, 2, D]), ("fxT", [P, 2, KT, P]), ("fz", [P, 2, P]), ("fzT", [P, 2, P]), ("f_top", [P, 2, 8]),
            ("f_ix", [P, 2, 8], mybir.dt.uint32), ("f_ixf", [P, 2, 8]), ("f_e", [P, 2, G2]), ("f_s", [P, 2, 2, G2]),
            ("f_w", [P, 2, G2]), ("f_r", [P, 2, 4]), ("fq", [P, 2, 3, D]))
        (gx, gxT, hid) = scope(("gx", [P, 2, GROUP, D]), ("gxT", [P, 2, KT, GROUP * P]), ("hid", [P, FT, GROUP * P]))
        (gx3, gxT3, lg, pe_, mk, rep, top, sm, mT, w2s) = scope(
            ("gx3", [P, 2, GROUP, D]), ("gxT3", [P, 2, KT, GROUP * P]),
            ("lg", [P, 2, P]), ("pe_", [P, 2, P]), ("mk", [P, 2, P]), ("rep", [P, P]), ("top", [P, 8]),
            ("sm", [P, 4]), ("mT", [P, 2, P]),
            ("w2s", [P, 2, CE, D]))
        w1s = [fcT[:, :, :], projT[:, :, :].rearrange("p (k c) n -> p k (c n)", k=KT)]
        w1b = rv_shift[0:1, :, :].rearrange("p (s b) n -> p s (b n)", s=2)
        w2b = attn_wT[0, "q"][0:1, :, :]
        h3 = [attn_wT[0, w][:, :, :].rearrange("p k n -> p (k n)") for w in "kv"]
        o3 = attn_wT[0, "o"][0:NB, :, :]
        m4, o4 = baseT[:, :, 0:P], attn_wT[1, "q"][:, :, :]

        names = """squares_loaded raw_loaded x_loaded const_ready set_tp set_ev set_amax set_red set_dve set_done
            set_pool set_wide set_tanh
            bn_done mv_ready veps_ready rstd_ready xn_ready bias_added x_added
            xT_done xT_ready qk_done v_done q_ready k_ready v_ready s_done max_done nm_ready hi_ready nm_hl_ready
            less_ready ex_ready t_done pT_ready hT_ready h_turned p_ready e0_ready o_done rec_ready mix_ready on_ready oT_done oT_ready
            y_done qu_ready qd_ready sT_ready r_done r_read ov_done ov_masked ov_summed ov_copied oh_done rel_done
            q2_ready q2_high_ready ov_turned mix2_ready fy_done quant_step route_in route_nm route_e route_step
            zw_ready zT_done zT_ready fxT_ready hid_done hid_ready lg_done lg_ready gxT_ready l3_step l3_e
            mk_ready f2_done wide_done mT_done
            mT_ready mg_done mg_ready h_done h_ready e_done e_ready fin_done""".split()
        S = {n: sem(n) for n in names}
        ctx_loaded = [sem(f"ctx_loaded{i}") for i in range(2)]
        km_loaded = [sem(f"km_loaded{i}") for i in range(2)]
        rv_loaded = sem("rv_loaded")
        row_loaded, q_stored, z_loaded = sem("row_loaded"), sem("q_stored"), sem("z_loaded")
        w1_loaded, w2_loaded = [[sem(f"{w}_loaded{i}") for i in range(2)] for w in ("w1", "w2")]
        o_stored = [sem(f"o_stored{i}") for i in range(2)]
        route_stored = sem("route_stored")
        mo_loaded = [sem(f"mo_loaded{i}") for i in range(2)]
        out_stored = sem("out_stored")

        def gate(st):
            i = st // 2 + 4 * (st % 2)
            return gates[:, i:i + 1]

        def xs(m, n=1):
            if n == 1:
                return x_all[:, m, :] if isinstance(m, int) else x_all[:, bass.ds(m, 1), :].squeeze(1)
            return x_all[:, m:m + n, :] if isinstance(m, int) else x_all[:, bass.ds(m, n), :]

        def over_samples(eng, step, lead=1):
            for b in range(-lead, 3):
                step(b, b % 2)
            with eng.Fori(3, NB - 4, 2) as b:
                step(b, 1)
                step(b + 1, 0)
            for b in range(NB - 3, NB + lead):
                step(b, b % 2)

        def exists(b):
            return not isinstance(b, int) or 0 <= b < NB

        def ln_stats(dve, st, m, s):
            n = NB * st + m
            if st == 0:
                dve.wait_ge(S["x_loaded"], 16 * (NB // 8))
            else:
                dve.wait_ge(S["x_added"], n - NB + 1)
            dve.bn_stats(bn6[:, s, :], xs(m)).then_inc(S["bn_done"], 1)
            dve.wait_ge(S["bn_done"], n + 1)
            wait(dve, S["rstd_ready"], n - 1)
            dve.memset(tick[:, 0:1], 0.0)
            dve.bn_aggr(mv[:, s, :], bn6[:, s, :]).then_inc(S["mv_ready"], 1)

        def ln_rstd(pool, st, m, s):
            n = NB * st + m
            pool.wait_ge(S["mv_ready"], n + 1)
            pool.tensor_tensor(veps[:, s:s + 1], mv[:, s, 1:2], eps_t[:, 0:1], ALU.add).then_inc(S["veps_ready"], 1)
            pool.wait_ge(S["veps_ready"], n + 1)
            wait(pool, S["xn_ready"], n - 1)
            pool.tensor_tensor(rstd[:, s:s + 1], veps[:, s:s + 1], eps_t[:, 1:2], ALU.pow)\
                .then_inc(S["rstd_ready"], 1)

        def ln_apply(dve, st, m, s, to, slots=2):
            n = NB * st + m
            dve.wait_ge(S["rstd_ready"], n + 1)
            wait(dve, S["xT_done"], n + 1 - slots)
            dve.tensor_scalar(to, xs(m), mv[:, s, 0:1], rstd[:, s:s + 1], ALU.subtract, ALU.mult)\
                .then_inc(S["xn_ready"], 1)

        def add_bias(pool, st, m):
            if st in HAS_BIAS:
                pool.wait_ge(S["xn_ready"], NB * st + m + 1)
                pool.tensor_tensor(xs(m), xs(m), bias_all[st][:, :], ALU.add).then_inc(S["bias_added"], 1)

        def wait_bias(dve, st, m):
            if st in HAS_BIAS:
                dve.wait_ge(S["bias_added"], NB * HAS_BIAS.index(st) + m + 1)
            else:
                dve.wait_ge(S["xn_ready"], NB * st + m + 1)

        sq_names = {"q": "Wq", "k": "Wk", "v": "Wv", "o": "Wo"}
        loads = []
        for i, (a, w) in enumerate(square):
            loads.append((raw_sq[:, i, :, :], A[f"L{a}_xattn_{sq_names[w]}"].rearrange("(m p) n -> p m n", p=P)))
        for w in "qkvo":
            src = A[f"L1_xattn_w_{w}"].rearrange("(k p) n -> p k n", p=P)
            loads.append(({"q": attn_wT[1, "q"], "o": attn_wT[1, "o"], "k": raw_k1, "v": raw_v1}[w][:, :, :], src))
        loads += [
            (raw_tern[:, :, :], A["L0_ffn_ternary_weight"].rearrange("(m p) n -> p m n", p=P)),
            (raw_base[:, :, :], A["L2_ffn_base_w"].rearrange("(m p) n -> p m n", p=P)),
            (raw_gl[:, :], A["L2_ffn_lora_A"].rearrange("e r d -> (e r) d")),
            (raw_g2[:, :], A["L2_ffn_gate_w"]),
            (raw_g3[:, :], A["L3_ffn_gate_w"]),
            (raw_fc[:, :, :], A["L1_ffn_W_fc"].rearrange("(m p) n -> p m n", p=P)),
            (raw_proj[:, :, :], A["L1_ffn_W_proj"].rearrange("(m p) n -> p m n", p=P)),
            (raw_bfc[:, :, :], A["L1_ffn_B_fc"].rearrange("(m p) r -> p m r", p=P)),
            (raw_bproj[:, :, :], A["L1_ffn_B_proj"].rearrange("(m p) r -> p m r", p=P)),
            (raw_afc[:, :], A["L1_ffn_A_fc"]),
            (raw_aproj[:, :], A["L1_ffn_A_proj"]),
            (raw_mask[:, :], A["mask_SxS2_if1"]),
            (b_fc[:, :], A["L1_ffn_b_fc"].rearrange("(t p) -> p t", p=P)),
        ]
        rk = A["L2_xattn_rk_table"]
        for a in range(8):
            first = P - HD + 1 - HD * a
            loads.append((raw_rk[:, 0, a, :], rk[first:first + P, :]))
            loads.append((raw_rk[0:HD - 1, 1, a, :], rk[first + P:first + RKW, :]))
        for m in range(KT):
            for e in range(E2):
                loads.append((raw_lb[:, m, e, :], A["L2_ffn_lora_B"][e, m * P:(m + 1) * P, :]))
        for i, a in enumerate((2, 3)):
            loads.append((bias_q[a][:, :], A[f"L{a}_xattn_bq"].rearrange("(t p) -> p t", p=P)))
            loads.append((bias_k[a][:, :], A[f"L{a}_xattn_bk"].rearrange("(t p) -> p t", p=P)))
            loads.append((bv_col[:, i, :], A[f"L{a}_xattn_bv"].rearrange("(t p) -> p t", p=P)))

        def spread(ap, n):
            return bass.AP(tensor=ap.tensor, offset=ap.offset, ap=[[0, P], [1, n]])

        for st, name in ((0, "L0_xattn_bo"), (1, "L0_ffn_bias"), (3, "L1_ffn_b_proj"), (4, "L2_xattn_bo"),
                         (5, "L2_ffn_base_b"), (6, "L3_xattn_bo")):
            loads.append((bias_all[st][:, :], spread(A[name], D)))
        loads.append((gates[:, 0:4], spread(A["g_xattn"], 4)))
        loads.append((gates[:, 4:8], spread(A["g_ffn"], 4)))
        loads.append((act_s[:, 0:1], spread(A["L0_ffn_act_scale"], 1)))
        for j in range(GROUP):
            loads.append((gate_b4[NE * j:NE * (j + 1), :], A["L3_ffn_gate_b"].rearrange("(e a) -> e a", a=1)))

        jobs = []
        for i, (a, w) in enumerate(square):
            jobs.append((attn_wT[a, w][:, :, :], P, KT * D,
                         [(raw_sq[:, i, m, k * P:(k + 1) * P], P, P, k * D + m * P) for k in range(KT) for m in range(KT)], 1.0))
        jobs.append((baseT[:, :, :], P, KT * D,
                     [(raw_base[:, m, k * P:(k + 1) * P], P, P, k * D + m * P) for k in range(KT) for m in range(KT)], 1.0))
        for k in range(KT):
            jobs.append((gateloraT[:, k, :], P, G2 + P,
                         [(raw_g2[:, k * P:(k + 1) * P], G2, P, 0), (raw_gl[:, k * P:(k + 1) * P], P, P, G2)], 1.0))
        jobs.append((gate3T[:, :, :], P, KT * NE,
                     [(raw_g3[:, k * P:(k + 1) * P], NE, P, k * NE) for k in range(KT)], 1.0))
        jobs.append((lora_bT[:, :], P, D,
                     [(raw_lb[:, m, :, :].rearrange("p e r -> p (e r)"), P, P, m * P) for m in range(KT)], 2.0))
        for c in range(FT // 4):
            jobs.append((lora_bfcT[:, c * SB:(c + 1) * SB], R, SB,
                         [(raw_bfc[:, 4 * c + i, :], P, R, i * P) for i in range(4)], 2.0))
        jobs.append((lora_bprojT[:, :], R, D, [(raw_bproj[:, i, :], P, R, i * P) for i in range(KT)], 2.0))
        N_EARLY = len(jobs)
        jobs.append((ternT[:, :, :], P, KT * D,
                     [(ternf[:, m, k * P:(k + 1) * P], P, P, k * D + m * P) for k in range(KT) for m in range(KT)], 1.0))
        jobs.append((rkT[:, :], P, RKW,
                     [(raw_rk[:, 0, :, :].rearrange("p a d -> p (a d)"), P, P, 0),
                      (raw_rk[0:HD - 1, 1, :, :].rearrange("p a d -> p (a d)"), HD - 1, P, P)], 1.0))
        N_MASKS = len(jobs)
        for k in range(KT):
            for c in range(FT // 4):
                jobs.append((fcT[:, k, c * SB:(c + 1) * SB], P, SB,
                             [(raw_fc[:, 4 * c + i, k * P:(k + 1) * P], P, P, i * P) for i in range(4)], 1.0))
        N_FC = len(jobs)
        for c in range(FT // 2):
            jobs.append((projT[:, 2 * c:2 * c + 2, :], P, 2 * D,
                         [(raw_proj[:, m, (2 * c + i) * P:(2 * c + i + 1) * P], P, P, i * D + m * P)
                          for i in range(2) for m in range(KT)], 1.0))
        adds = []
        for k in range(KT):
            for c in range(FT // 4):
                adds.append((fcT[:, k, c * SB:(c + 1) * SB], SB,
                             [(raw_afc[:, k * P:(k + 1) * P], lora_bfcT[:, c * SB:(c + 1) * SB])]))
        for t in range(FT):
            adds.append((projT[:, t, :], D, [(raw_aproj[:, t * P:(t + 1) * P], lora_bprojT[:, :])]))
        for i, (st, a) in enumerate(((4, 2), (6, 3))):
            adds.append((bias_all[st][:, :], D,
                         [(bv_rep[:, i, k, :], attn_wT[a, "o"][:, k, :]) for k in range(KT)]))
        RAW = 16 * (len(loads) - len(square))
        VEC_EARLY, VEC_FC, VEC_PROJ = [0], [0], [0]

        def setup_loads(sp):
            for i, (dst, src) in enumerate(loads):
                sp.dma_start(dst, src, allow_slow_non_contiguous=True)\
                  .then_inc(S["squares_loaded" if i < len(square) else "raw_loaded"], 16)
            for m in range(0, NB, 8):
                if m == NB - FREE:
                    sp.wait_ge(S["set_ev"], len(square))
                sp.dma_start(x_all[:, m:m + 8, :], A["x"][m:m + 8].rearrange("b p d -> p b d")).then_inc(S["x_loaded"], 16)
            rv = A["L2_xattn_rv_table"]
            for b in range(HD):
                sp.dma_start(rv_shift[:, b, :].rearrange("p (a d) -> p a d", d=HD),
                             bass.AP(tensor=rv.tensor, offset=rv.offset + (b + 1) * HD,
                                     ap=[[HD, P], [HD * HD, 8], [1, HD]])).then_inc(rv_loaded, 16)

        def setup_pool(pool):
            count = [0]

            def then(ins):
                count[0] += 1
                ins.then_inc(S["set_pool"], 1)
                pool.wait_ge(S["set_pool"], count[0])

            def select(t, pattern, cm, op, fill, base=0):
                then(pool.affine_select(out=t, in_=t, pattern=pattern, compare_op=op, fill=fill, base=base,
                                        channel_multiplier=cm))
            for t, v in ((ones_b, 1.0), (ident, 0.0), (ident_b, 0.0), (causal_q, 0.0), (later_k, 1.0),
                         (block8, 1.0), (block8r, 1.0), (place16, 0.0), (floor, 0.0)):
                then(pool.memset(t[:, :], v))
            then(pool.memset(eps_t[:, 0:1], EPS))
            then(pool.memset(eps_t[:, 1:2], -0.5))
            for t in (ident, ident_b):
                select(t[:, :], [[-1, P]], 1, ALU.not_equal, 1.0)
            select(causal_q[:, :], [[-1, P]], 1, ALU.is_ge, -BIG)
            select(later_k[:, :], [[-1, P]], 1, ALU.is_gt, 0.0)
            select(floor[:, :], [[0, 1]], 1, ALU.not_equal, -BIG, base=-(P - 1))
            select(block8[:, :], [[-HD, 8]], 1, ALU.is_ge, 0.0)
            select(block8[:, :], [[HD, 8]], -1, ALU.is_ge, 0.0, base=HD - 1)
            select(block8r[:, :], [[HD, 8]], 1, ALU.is_ge, 0.0, base=-7 * HD)
            select(block8r[:, :], [[-HD, 8]], -1, ALU.is_ge, 0.0, base=8 * HD - 1)
            then(pool.iota(iota_i[:, :], pattern=[[1, G2]], base=0, channel_multiplier=0))
            pool.memset(ones[:, :], 1.0).then_inc(S["const_ready"], 1)
            for i in range(2):
                pool.wait_ge(S["set_amax"], i + 1)
                pool.partition_all_reduce(amax[:, 2 + i:3 + i], amax[:, i:i + 1], P, RMAX).then_inc(S["set_red"], 1)

        def setup_act(act):
            for j, (dst, rows, cols, _, scale) in enumerate(jobs):
                if j == len(square):
                    act.wait_ge(S["raw_loaded"], RAW)
                    act.activation(gates[:, :], gates[:, :], ACT.Tanh).then_inc(S["set_tanh"], 1)
                act.wait_ge(S["set_tp"], j + 1)
                src = ps[0:rows, j % 8, 0:cols]
                if len(dst.shape) == 3:
                    src = src.rearrange("p (a n) -> p a n", a=dst.shape[1])
                act.mul(dst, src, scale).then_inc(S["set_ev"], 1)

        def setup_pe(pe):
            pe.wait_ge(S["const_ready"], 1)
            pe.wait_ge(S["squares_loaded"], 16 * len(square))
            for j, (_, _, _, parts, _) in enumerate(jobs):
                if j == len(square):
                    pe.wait_ge(S["raw_loaded"], RAW)
                if j == N_EARLY:
                    pe.wait_ge(S["set_dve"], VEC_EARLY[0])
                if j == N_MASKS:
                    pe.wait_ge(S["set_dve"], VEC_FC[0])
                if j == N_FC:
                    pe.wait_ge(S["set_dve"], VEC_PROJ[0])
                wait(pe, S["set_ev"], j - 7)
                for i, (src, rows, cols, at) in enumerate(parts):
                    last = pe.transpose(ps[0:cols, j % 8, at:at + rows], src, ident[0:rows, 0:rows])
                last.then_inc(S["set_tp"], 1)
            pe.wait_ge(S["set_ev"], len(jobs))
            for j, (_, cols, parts) in enumerate(adds):
                wait(pe, S["set_wide"], j - 7)
                for i, (lhsT, rhs) in enumerate(parts):
                    last = pe.matmul(ps[:, j % 8, 0:cols], lhsT, rhs, start=(i == 0), stop=(i == len(parts) - 1))
                last.then_inc(S["set_tp"], 1)

        def setup_dve(dve):
            count = [0]

            def then(ins):
                count[0] += 1
                ins.then_inc(S["set_dve"], 1)
                dve.wait_ge(S["set_dve"], count[0])

            dve.wait_ge(S["const_ready"], 1)
            then(dve.tensor_reduce(parity[:, :], block8[:, :].rearrange("p (g two) -> p two g", two=2), AX.X, ALU.add))
            then(dve.tensor_reduce(mod16[:, :], ident[:, :].rearrange("p (r i) -> p i r", i=HD), AX.X, ALU.add))
            then(dve.tensor_copy(place16[:, HD:2 * HD], mod16[:, :]))
            then(dve.tensor_copy(iota10[:, :], iota_i[:, :]))
            dve.wait_ge(S["raw_loaded"], RAW)
            then(dve.tensor_scalar(ternf[:, :, :], raw_tern[:, :, :], -1.0, None, ALU.add))
            then(dve.tensor_scalar(am_f[:, :], raw_mask[:, :], 0.0, -BIG, ALU.is_equal, ALU.mult))
            VEC_EARLY[0] = count[0]
            then(dve.tensor_copy(given_q[:, :], am_f[:, :]))
            then(dve.tensor_reduce(am_any[:, 0:1], am_f[:, :], AX.X, ALU.max))
            then(dve.tensor_scalar(am_any[:, 0:1], am_any[:, 0:1], 0.0, None, ALU.is_equal))
            then(dve.reciprocal(am_any[:, 1:2], am_any[:, 0:1]))
            then(dve.tensor_tensor(row_ok[:, :], am_any[:, 0:1], am_any[:, 1:2], ALU.mult))
            for k in range(KT):
                for w, src in (("k", raw_k1), ("v", raw_v1)):
                    then(dve.tensor_copy(attn_wT[1, w][:, k, :].rearrange("p (h d) -> p h d", d=HD), bc(src[:, k, :], H, 1)))
            for t in range(KT):
                then(dve.tensor_scalar(bias_qp[:, t, :], parity[:, :], bias_q[3][:, t:t + 1], None, ALU.mult))
            then(dve.tensor_copy(bv_rep[:, :, :, :], bc(bv_col[:, :, :], P, 3)))
            flat = [raw_fc[:, :, :].rearrange("p m n -> p (m n)"), raw_proj[:, :, :].rearrange("p m n -> p (m n)")]
            for i, w in enumerate(flat):
                dve.tensor_reduce(amax[:, i:i + 1], w, AX.X, ALU.max, apply_absolute_value=True).then_inc(S["set_amax"], 1)
            for i, w in enumerate(flat):
                dve.wait_ge(S["set_red"], i + 1)
                scale, inv = amax[:, 4 + i:5 + i], amax[:, 6 + i:7 + i]
                then(dve.tensor_scalar(scale, amax[:, 2 + i:3 + i], 1.0 / QB, None, ALU.mult))
                then(dve.reciprocal(inv, scale))
                then(dve.tensor_scalar(quant[:, :], w, inv, ROUND, ALU.mult, ALU.add))
                then(dve.tensor_scalar(quant[:, :], quant[:, :], -ROUND, QB, ALU.add, ALU.min))
                then(dve.tensor_scalar(quant[:, :], quant[:, :], -QB - 1.0, scale, ALU.max, ALU.mult))
                then(dve.tensor_tensor(quant2[:, :], quant[:, :], w, ALU.subtract))
                then(dve.tensor_tensor(w, quant2[:, :], w, ALU.add))
                (VEC_FC, VEC_PROJ)[i][0] = count[0]
            then(dve.tensor_scalar(act_s[:, 0:1], act_s[:, 0:1], EPS, 3e38, ALU.max, ALU.min))
            then(dve.reciprocal(act_s[:, 1:2], act_s[:, 0:1]))
            dve.wait_ge(S["set_tanh"], 1)
            then(dve.tensor_tensor(act_s[:, 2:3], act_s[:, 0:1], gate(1), ALU.mult))
            for j, (dst, cols, _) in enumerate(adds):
                dve.wait_ge(S["set_tp"], len(jobs) + j + 1)
                dve.tensor_tensor(dst, ps[:, j % 8, 0:cols], dst, ALU.add).then_inc(S["set_wide"], 1)
            dve.wait_ge(S["set_wide"], len(adds))
            for st in HAS_BIAS:
                then(dve.tensor_scalar(bias_all[st][:, :], bias_all[st][:, :], gate(st), None, ALU.mult))
            dve.wait_ge(S["set_ev"], len(jobs))
            dve.memset(v1[:, :, :, HD + 1:VW], 0.0)
            dve.memset(v1[:, :, :, HD:HD + 1], 1.0).then_inc(S["set_done"], 1)

        def place(h):
            return h % 8 // 2 * 4 + h // 8 * 2 + h % 2

        def turn_weighed(pe):
            for g in range(4):
                last = pe.transpose(ps[:, 7, g * P:(g + 1) * P], headT[:, g * P:(g + 1) * P], ident[:, :])
            return last

        def attention_sp(sp, a):
            def load(m, s):
                n = NB * a + m
                sp.wait_ge(S["xT_done"], NB * 2 * a + m - 1)
                sp.dma_start(ctx_raw[:, s, :], A["ctx_1024"][m] if isinstance(m, int) else
                             A["ctx_1024"][bass.ds(m, 1)].squeeze(0)).then_inc(ctx_loaded[s], 16)
                if a == 0:
                    wait(sp, S["k_ready"], n - 1)
                    row = A["mask_BxS2_ff1"]
                    sp.dma_start(key_scale[:, s, :], bass.AP(tensor=row.tensor, offset=row.offset + m * P,
                                                             ap=[[0, P], [1, P]])).then_inc(km_loaded[s], 16)
            for m in range(2):
                if a:
                    sp.wait_ge(S["xT_done"], NB * 2 * (a - 1) + NB - 1 + m)
                load_first(sp, a, m)
            with sp.Fori(2, NB - 1, 2) as m:
                load(m, 0)
                load(m + 1, 1)

        def load_first(sp, a, m):
            sp.dma_start(ctx_raw[:, m, :], A["ctx_1024"][m]).then_inc(ctx_loaded[m], 16)
            if a == 0:
                row = A["mask_BxS2_ff1"]
                sp.dma_start(key_scale[:, m, :], bass.AP(tensor=row.tensor, offset=row.offset + m * P,
                                                         ap=[[0, P], [1, P]])).then_inc(km_loaded[m], 16)

        def slot_count(a, m, s):
            return NB // 2 * a * 16 + 16 + 8 * (m - s)

        def attention_pe(pe, a):
            st = 2 * a
            additive = given_q if a == 3 else causal_q

            def N(m):
                return NB * a + m

            def M(m):
                return NB * min(a, 2) + m

            def transpose_in(m, s):
                pe.wait_ge(S["xn_ready"], NB * st + m + 1)
                pe.wait_ge(ctx_loaded[s], slot_count(a, m, s))
                wait(pe, S["x_added"], NB * st + m - 2)
                wait(pe, S["xT_ready"], NB * (st // 2) + m)
                for k in range(KT):
                    pe.transpose(ps[:, 4, k * P:(k + 1) * P], xn[:, s, k * P:(k + 1) * P], ident[:, :])
                for k in range(KT):
                    last = pe.transpose(ps[:, 4, (KT + k) * P:(KT + k + 1) * P], ctx_raw[:, s, k * P:(k + 1) * P],
                                        ident[:, :])
                last.then_inc(S["xT_done"], 1)

            def project_qk(m, s):
                pe.wait_ge(S["xT_ready"], NB * (st // 2) + m + 1)
                wait(pe, S["q_ready"], M(m))
                wait(pe, S["k_ready"], N(m))
                for o, w in ((0, "q"), (KT, "k")):
                    for t in range(KT):
                        for k in range(KT):
                            last = pe.matmul(ps[:, 5, (o + t) * P:(o + t + 1) * P],
                                             attn_wT[a, w][:, k, t * P:(t + 1) * P], xcT[:, s, o + k, :],
                                             start=(k == 0), stop=(k == KT - 1))
                last.then_inc(S["qk_done"], 1)

            def project_v(m, s):
                wait(pe, S["v_ready"], N(m))
                for k in range(KT):
                    last = pe.matmul(ps[:, 6, 0:D], xcT[:, s, KT + k, :], attn_wT[a, "v"][:, k, :],
                                     start=(k == 0), stop=(k == KT - 1))
                last.then_inc(S["v_done"], 1)

            def score(b, s):
                pe.wait_ge(S["q_ready"], M(b) + 1)
                pe.wait_ge(S["k_ready"], N(b) + 1)
                for pair in range(2):
                    wait(pe, S["pT_ready"], 2 * M(b) - 1 + pair)
                    for g in (2 * pair, 2 * pair + 1):
                        pe.matmul(ps[:, g, :], ident_b[:, :], bc(additive[:, :], 4, 1), start=True, stop=True)
                    for j in range(4):
                        for g in (2 * pair, 2 * pair + 1):
                            rows = slice(32 * g, 32 * g + 32)
                            last = pe.matmul(ps[:, g, j * P:(j + 1) * P], qm[rows, s, j % 2, j // 2, :],
                                             kT[rows, s, j // 2, :], start=False, stop=True, skip_group_check=True)
                    last.then_inc(S["s_done"], 1)

            def turn_probs(b, half):
                pe.wait_ge(S["ex_ready"], 2 * M(b) + half + 1)
                for i in range(8 * half, 8 * half + 8):
                    last = pe.transpose(ps[:, i // 4, i % 4 * P:(i % 4 + 1) * P], exps[:, i * P:(i + 1) * P],
                                        ident[:, :])
                last.then_inc(S["t_done"], 1)

            def weigh(b, s):
                pe.wait_ge(S["pT_ready"], 2 * M(b) + 2)
                pe.wait_ge(S["v_ready"], N(b) + 1)
                wait(pe, S["oT_ready"], N(b))
                for h in range(H):
                    last = pe.matmul(ps[VW * (h % 4):VW * (h % 4 + 1), 7, h // 4 * P:(h // 4 + 1) * P],
                                     v1[:, s, h, :], probsT[:, place(h) * P:(place(h) + 1) * P], start=True, stop=True)
                if a == 0:
                    wait(pe, S["x_added"], b)
                    if exists(b + 2):
                        pe.wait_ge(S["xT_ready"], b + 3)
                    last = pe.matmul(ps[:, 4, 0:H * (HD + 1)], later_k[:, :], v1[:, s, :, 0:HD + 1],
                                     start=True, stop=True)
                last.then_inc(S["o_done"], 1)

            def turn_heads(b):
                pe.wait_ge(S["hT_ready"], N(b) + 1)
                turn_weighed(pe).then_inc(S["h_turned"], 1)

            def transpose_out(b, s):
                pe.wait_ge(S["on_ready"], N(b) + 1)
                for k in range(KT):
                    last = pe.transpose(ps[:, 7, k * P:(k + 1) * P], on[:, s, k * P:(k + 1) * P], ident[:, :])
                last.then_inc(S["oT_done"], 1)

            def project_out(b, s):
                pe.wait_ge(S["oT_ready"], N(b) + 1)
                for k in range(KT):
                    last = pe.matmul(ps[:, 4, 0:D], oT[:, s, k, :], attn_wT[a, "o"][:, k, :], start=(k == 0),
                                     stop=(k == KT - 1))
                last.then_inc(S["y_done"], 1)

            def step(b, s):
                o = 1 - s
                if exists(b):
                    score(b, s)
                if exists(b + 1):
                    transpose_in(b + 1, o)
                if exists(b - 1):
                    weigh(b - 1, o)
                if exists(b + 1):
                    project_qk(b + 1, o)
                if exists(b - 1):
                    turn_heads(b - 1)
                if exists(b + 1):
                    project_v(b + 1, o)
                if exists(b):
                    turn_probs(b, 0)
                if exists(b - 1):
                    transpose_out(b - 1, o)
                if exists(b):
                    turn_probs(b, 1)
                if exists(b - 1):
                    project_out(b - 1, o)
            over_samples(pe, step)

        def attention_act(act, a):
            st = 2 * a

            def N(m):
                return NB * a + m

            def M(m):
                return NB * min(a, 2) + m

            def exponentiate(b, half):
                act.wait_ge(S["less_ready"], 2 * M(b) + half + 1)
                cols = exps[:, half * 8 * P:(half + 1) * 8 * P]
                act.activation(cols, cols, ACT.Exp, scale=SCALE).then_inc(S["ex_ready"], 1)

            def step(b, s):
                o = 1 - s
                if exists(b + 1):
                    act.wait_ge(S["xT_done"], NB * st + b + 2)
                    wait(act, S["v_done"], N(b))
                    act.copy(xcT[:, o, :, :], ps[:, 4, :].rearrange("p (k n) -> p k n", k=2 * KT))\
                       .then_inc(S["xT_ready"], 1)
                if exists(b - 1):
                    act.wait_ge(S["o_done"], N(b))
                    wait(act, S["h_turned"], N(b) - 1)
                    act.copy(headT[:, :], ps[:, 7, :]).then_inc(S["hT_ready"], 1)
                if exists(b):
                    exponentiate(b, 0)
                    exponentiate(b, 1)
                    if a == 0:
                        wait(act, S["on_ready"], b - 1)
                        act.activation(e0[:, s, :].rearrange("q (t g p) -> q g t p", t=2, g=4),
                                       nm[:, s, :].rearrange("q (g t p) -> q g t p", t=2, g=4), ACT.Exp, scale=-SCALE)\
                           .then_inc(S["e0_ready"], 1)
                if exists(b + 1):
                    act.wait_ge(S["qk_done"], N(b) + 2)
                    wait(act, S["s_done"], 2 * M(b))
                    for p in range(2):
                        if a == 3:
                            for t in range(KT):
                                ins = act.activation(qm[:, o, p, t, :], ps[:, 5, t * P:(t + 1) * P], ACT.Identity,
                                                     bias=bias_qp[:, t, p:p + 1], scale=parity[:, p:p + 1])
                                if p and t:
                                    ins.then_inc(S["q_ready"], 1)
                        else:
                            ins = act.mul(qm[:, o, p, :, :], ps[:, 5, 0:D].rearrange("p (t n) -> p t n", t=KT),
                                          parity[:, p:p + 1])
                            if p:
                                ins.then_inc(S["q_ready"], 1)
                    if a == 3:
                        act.activation(kT[:, o, 0, :], ps[:, 5, D:D + P], ACT.Identity, bias=bias_k[3][:, 0:1])
                        act.activation(kT[:, o, 1, :], ps[:, 5, D + P:D + 2 * P], ACT.Identity,
                                       bias=bias_k[3][:, 1:2]).then_inc(S["k_ready"], 1)
                    elif a == 1:
                        act.copy(kT[:, o, :, :], ps[:, 5, D:2 * D].rearrange("p (t n) -> p t n", t=KT))\
                           .then_inc(S["k_ready"], 1)
                if exists(b):
                    wait(act, S["o_done"], N(b))
                    for half in range(2):
                        act.wait_ge(S["t_done"], 2 * M(b) + half + 1)
                        act.copy(probsT[:, half * 8 * P:(half + 1) * 8 * P],
                                 ps[:, 2 * half:2 * half + 2, :].rearrange("p g n -> p (g n)")).then_inc(S["pT_ready"], 1)
            if a == 0:
                act.wait_ge(S["set_done"], 1)
            over_samples(act, step)

        def attention_dve(dve, a):
            st = 2 * a

            def N(m):
                return NB * a + m

            def M(m):
                return NB * min(a, 2) + m

            def prologue():
                for m in (0, 1):
                    ln_stats(dve, st, m, m)
                    ln_apply(dve, st, m, m, xn[:, m, :])
                ln_stats(dve, st, 2, 0)

            def step(b, s):
                o = 1 - s
                if exists(b):
                    if a == 0:
                        wait(dve, S["e0_ready"], b - 1)
                    for half in range(2):
                        dve.wait_ge(S["s_done"], 2 * M(b) + half + 1)
                        dve.tensor_reduce(nm[:, s, 8 * half:8 * half + 8],
                                          ps[:, 2 * half:2 * half + 2, :].rearrange("p g (j n) -> p (g j) n", n=P), AX.X,
                                          ALU.max).then_inc(S["max_done"], 1)
                    dve.wait_ge(S["max_done"], 2 * M(b) + 2)
                    if a == 0:
                        dve.tensor_scalar(nm[:, s, :], nm[:, s, :], floor[:, :], None, ALU.max).then_inc(S["nm_ready"], 1)
                        dve.wait_ge(S["nm_ready"], b + 1)
                    wait(dve, S["t_done"], 2 * M(b))
                    for half in range(2):
                        dve.tensor_tensor(exps[:, half * 8 * P:(half + 1) * 8 * P].rearrange("p (i n) -> p i n", n=P),
                                          ps[:, 2 * half:2 * half + 2, :].rearrange("p g (j n) -> p (g j) n", n=P),
                                          bc(nm[:, s, 8 * half:8 * half + 8], P, 2), ALU.subtract)\
                           .then_inc(S["less_ready"], 1)
                if exists(b - 1):
                    normalise(b - 1, o)
                if exists(b + 1):
                    dve.wait_ge(S["v_done"], N(b) + 2)
                    wait(dve, S["o_done"], N(b))
                    dve.tensor_copy(v1[:, o, :, 0:HD], ps[:, 6, 0:D].rearrange("p (h d) -> p h d", d=HD))\
                       .then_inc(S["v_ready"], 1)
                    if a == 0:
                        dve.wait_ge(S["q_ready"], M(b) + 2)
                        dve.wait_ge(km_loaded[o], slot_count(0, b + 1, o))
                        wait(dve, S["s_done"], 2 * M(b))
                        dve.tensor_tensor(kT[:, o, :, :], ps[:, 5, D:2 * D].rearrange("p (t n) -> p t n", t=KT),
                                          bc(key_scale[:, o, :], KT, 1), ALU.mult).then_inc(S["k_ready"], 1)
                if exists(b - 1):
                    dve.wait_ge(S["oT_done"], N(b))
                    wait(dve, S["y_done"], N(b) - 2)
                    dve.tensor_copy(oT[:, o, :, :], ps[:, 7, 0:D].rearrange("p (k n) -> p k n", k=KT))\
                       .then_inc(S["oT_ready"], 1)
                    dve.wait_ge(S["y_done"], N(b))
                    wait_bias(dve, st, b - 1)
                    dve.scalar_tensor_tensor(xs(b - 1), ps[:, 4, 0:D], gate(st), xs(b - 1), ALU.mult, ALU.add)\
                       .then_inc(S["x_added"], 1)
                if exists(b + 2) and not (isinstance(b, int) and b < 0):
                    ln_apply(dve, st, b + 2, s, xn[:, s, :])
                if exists(b + 3) and not (isinstance(b, int) and b < 0):
                    ln_stats(dve, st, b + 3, o)

            def normalise(b, s):
                dve.wait_ge(S["h_turned"], N(b) + 1)
                heads = ps[:, 7, :].rearrange("p (h d) -> p h d", d=VW)[:, :, 0:HD + 1]
                if a == 0:
                    dve.wait_ge(S["e0_ready"], b + 1)
                    dve.tensor_tensor(mix[:, :, :], ps[:, 4, 0:H * (HD + 1)].rearrange("p (h d) -> p h d", d=HD + 1),
                                      bc(e0[:, s, :], HD + 1, 2), ALU.mult).then_inc(S["mix_ready"], 1)
                    dve.wait_ge(S["mix_ready"], 2 * b + 1)
                    dve.tensor_tensor(mix[:, :, :], heads, mix[:, :, :], ALU.add).then_inc(S["mix_ready"], 1)
                    dve.wait_ge(S["mix_ready"], 2 * b + 2)
                    heads = mix[:, :, :]
                dve.reciprocal(rec[:, s, :], heads[:, :, HD]).then_inc(S["rec_ready"], 1)
                done = N(b) + 1 if a < 3 else 3 * NB + 2 * b + 1
                dve.wait_ge(S["rec_ready"], done)
                if a == 3:
                    dve.tensor_scalar(rec[:, s, :], rec[:, s, :], row_ok[:, :], None, ALU.mult)\
                       .then_inc(S["rec_ready"], 1)
                    dve.wait_ge(S["rec_ready"], done + 1)
                wait(dve, S["oT_done"], N(b) - 1)
                dve.tensor_tensor(on[:, s, :].rearrange("p (h d) -> p h d", d=HD), heads[:, :, 0:HD],
                                  bc(rec[:, s, :], HD, 2), ALU.mult).then_inc(S["on_ready"], 1)
            prologue()
            over_samples(dve, step)

        def N2(m):
            return NB * 2 + m

        def by_head(ap):
            return ap.rearrange("p (h a b) -> p b a h", b=HD, a=8)

        def of_head(ap, h):
            return ap[:, h * P:(h + 1) * P]

        def shifted_sp(sp):
            def load(m, s):
                sp.wait_ge(S["xT_done"], NB * 4 + m - 1)
                sp.dma_start(ctx_raw[:, s, :], A["ctx_1024"][m] if isinstance(m, int) else
                             A["ctx_1024"][bass.ds(m, 1)].squeeze(0)).then_inc(ctx_loaded[s], 16)

            def maxima(b, s):
                sp.wait_ge(S["nm_hl_ready"], b + 1)
                wait(sp, S["oh_done"], b)
                for c in range(2):
                    sp.dma_start(nm_row[c:c + 1, :].rearrange("c (q h) -> c q h", h=H), nm_hl[:, 0, c:c + 1, :])\
                      .then_inc(row_loaded, 16)

            def queries(m, s):
                sp.wait_ge(S["qu_ready"], m + 1)
                sp.dma_start(query_dram[s].rearrange("(t p) n -> p t n", p=P), qu[:, s, :, :]).then_inc(q_stored, 16)
                sp.wait_ge(q_stored, 16 * m + 16)
                wait(sp, S["q2_high_ready"], m)
                wait(sp, S["q2_ready"], m)
                for a in range(8):
                    sp.dma_start(qz[HD * a:HD * (a + 1), :, :],
                                 query_dram[s].rearrange("(h d) (a b) -> a d h b", d=HD, b=HD)[a]).then_inc(z_loaded, 16)

            def step(b, s):
                if exists(b):
                    maxima(b, s)
                if exists(b + 1):
                    queries(b + 1, 1 - s)
                if exists(b + 3) and not (isinstance(b, int) and b < -1):
                    load(b + 3, 1 - s)
            for m in range(2):
                sp.wait_ge(S["xT_done"], NB * 2 + NB - 1 + m)
                load_first(sp, 2, m)
            over_samples(sp, step)

        def shifted_pe(pe):
            a, st = 2, 4

            def transpose_in(m, s):
                pe.wait_ge(S["xn_ready"], NB * st + m + 1)
                pe.wait_ge(ctx_loaded[s], slot_count(a, m, s))
                wait(pe, S["x_added"], NB * st + m - 2)
                for k in range(KT):
                    pe.transpose(ps[:, 4, k * P:(k + 1) * P], xn[:, s, k * P:(k + 1) * P], ident[:, :])
                for k in range(KT):
                    last = pe.transpose(ps[:, 4, (KT + k) * P:(KT + k + 1) * P], ctx_raw[:, s, k * P:(k + 1) * P],
                                        ident[:, :])
                last.then_inc(S["xT_done"], 1)

            def project(m, s):
                pe.wait_ge(S["xT_ready"], NB * (st // 2) + m + 1)
                wait(pe, S["r_read"], 4 * m)
                for o, w in ((0, "q"), (KT, "k")):
                    for t in range(KT):
                        for k in range(KT):
                            last = pe.matmul(ps[:, 5, (o + t) * P:(o + t + 1) * P],
                                             attn_wT[a, w][:, k, t * P:(t + 1) * P], xcT[:, s, o + k, :],
                                             start=(k == 0), stop=(k == KT - 1))
                last.then_inc(S["qk_done"], 1)
                for k in range(KT):
                    last = pe.matmul(ps[:, 6, 0:D], xcT[:, s, KT + k, :], attn_wT[a, "v"][:, k, :],
                                     start=(k == 0), stop=(k == KT - 1))
                last.then_inc(S["v_done"], 1)

            def score_keys(b, s, banks):
                if banks[0] == 0:
                    pe.wait_ge(S["qd_ready"], 2 * (b + 1))
                    pe.wait_ge(S["k_ready"], N2(b) + 1)
                    wait(pe, S["p_ready"], b)
                for g in banks:
                    for t in range(KT):
                        cols = ps[:, g, :].rearrange("p (c t h) -> p c t h", t=KT, h=8)[:, :, t, :]
                        pe.matmul(cols, kT[:, s, t, :],
                                  qd[:, 4 * g:4 * g + 4, :, :].rearrange("p b a (t h) -> p (b a) t h", t=KT)[:, :, t, :],
                                  start=(t == 0), stop=True, skip_group_check=True)

            def score_offsets(b, s):
                pe.wait_ge(S["q2_ready"], b + 1)
                pe.wait_ge(S["q2_high_ready"], b + 1)
                for i in range(HD):
                    last = pe.matmul(ps[:, i // 4, i % 4 * P:(i % 4 + 1) * P], rkT[:, HD - 1 - i:HD - 1 - i + P],
                                     q2[:, i, :, :].rearrange("p a h -> p (a h)"), start=False, stop=True,
                                     skip_group_check=True)
                last.then_inc(S["rel_done"], 1)

            def turn_scores(b, part):
                pe.wait_ge(S["sT_ready"], b + 1)
                pe.wait_ge(S["v_ready"], N2(b) + 1)
                for c in (2 * part, 2 * part + 1):
                    if c >= 2:
                        pe.wait_ge(S["r_read"], 4 * b + c - 1)
                    for j in range(4):
                        last = pe.transpose(ps[:, 5 + c % 2, j * P:(j + 1) * P], of_head(sT[:, :], 4 * c + j), ident[:, :])
                    last.then_inc(S["r_done"], 1)

            def subtract_maxima(b, s):
                pe.wait_ge(row_loaded, 32 * b + 32)
                for g in range(4):
                    last = pe.matmul(ps[:, g, :], ones_b[:, :],
                                     nm_row[:, :].rearrange("c (a b h) -> c b a h", a=8, b=HD)[:, 4 * g:4 * g + 4, :, :],
                                     start=False, stop=True,
                                     skip_group_check=True)
                last.then_inc(S["oh_done"], 1)

            def weigh(b, s):
                pe.wait_ge(S["p_ready"], b + 1)
                pe.wait_ge(S["v_ready"], N2(b) + 1)
                wait(pe, S["on_ready"], N2(b))
                for h in range(H):
                    last = pe.matmul(ps[VW * (h % 4):VW * (h % 4 + 1), 7, h // 4 * P:(h // 4 + 1) * P],
                                     v1[:, s, h, :], of_head(probs[:, s, :], h), start=True, stop=True)
                last.then_inc(S["o_done"], 1)

            def weigh_offsets(b, s, part):
                for c in (2 * part, 2 * part + 1):
                    if c >= 2:
                        pe.wait_ge(S["ov_masked"], 4 * b + c - 1)
                    elif exists(b + 2):
                        pe.wait_ge(S["qu_ready"], b + 3)
                        pe.wait_ge(S["k_ready"], N2(b) + 3)
                        if c == 1:
                            pe.wait_ge(S["v_ready"], N2(b) + 3)
                    elif exists(b + 1):
                        pe.wait_ge(S["r_read"], 4 * b + 8)
                    for i in range(4):
                        last = pe.matmul(ps[:, 5 + c % 2, i * P:(i + 1) * P], rv_shift[:, HD - 1 - 4 * c - i, :],
                                         by_head(probs[:, s, :])[:, 4 * c + i, :, :], start=True, stop=True)
                    last.then_inc(S["ov_done"], 1)

            def sum_offsets(b, s):
                pe.wait_ge(S["ov_masked"], 4 * b + 4)
                if exists(b + 2):
                    pe.wait_ge(S["xT_ready"], NB * (st // 2) + b + 3)
                wait(pe, S["x_added"], NB * st + b)
                for t in range(KT):
                    for p in range(2):
                        for j in range(4):
                            last = pe.matmul(ps[32 * j:32 * (j + 1), 4, D + t * P:D + (t + 1) * P],
                                             place16[:, HD - HD * p:3 * HD - HD * p],
                                             of_head(spread_v[:, :], 8 * t + 2 * j + p), start=(p == 0), stop=(p == 1),
                                             skip_group_check=True)
                last.then_inc(S["ov_summed"], 1)

            def turn_offsets(b, s):
                pe.wait_ge(S["ov_copied"], b + 1)
                for k in range(KT):
                    last = pe.transpose(ps[:, 4, k * P:(k + 1) * P], ovT[:, k * P:(k + 1) * P], ident[:, :])
                last.then_inc(S["ov_turned"], 1)

            def transpose_out(b, s):
                pe.wait_ge(S["on_ready"], N2(b) + 1)
                for k in range(KT):
                    last = pe.transpose(ps[:, 6, k * P:(k + 1) * P], on[:, s, k * P:(k + 1) * P], ident[:, :])
                last.then_inc(S["oT_done"], 1)

            def project_out(b, s):
                pe.wait_ge(S["oT_ready"], N2(b) + 1)
                for k in range(KT):
                    last = pe.matmul(ps[:, 4, 0:D], oT[:, s, k, :], attn_wT[a, "o"][:, k, :], start=(k == 0),
                                     stop=(k == KT - 1))
                last.then_inc(S["y_done"], 1)

            def step(b, s):
                o = 1 - s
                if exists(b):
                    score_offsets(b, s)
                if exists(b - 1):
                    weigh(b - 1, o)
                if exists(b):
                    turn_scores(b, 0)
                if exists(b + 1):
                    transpose_in(b + 1, o)
                if exists(b):
                    turn_scores(b, 1)
                if exists(b - 1):
                    pe.wait_ge(S["hT_ready"], N2(b))
                    turn_weighed(pe).then_inc(S["h_turned"], 1)
                if exists(b + 1):
                    project(b + 1, o)
                if exists(b - 1):
                    weigh_offsets(b - 1, o, 0)
                if exists(b):
                    subtract_maxima(b, s)
                if exists(b - 1):
                    weigh_offsets(b - 1, o, 1)
                    sum_offsets(b - 1, o)
                if exists(b + 1):
                    score_keys(b + 1, o, (0,))
                if exists(b - 1):
                    turn_offsets(b - 1, o)
                if exists(b + 1):
                    score_keys(b + 1, o, (1, 2))
                if exists(b - 1):
                    transpose_out(b - 1, o)
                if exists(b + 1):
                    score_keys(b + 1, o, (3,))
                if exists(b - 1):
                    project_out(b - 1, o)
            pe.wait_ge(rv_loaded, 16 * HD)
            over_samples(pe, step)

        def shifted_act(act):
            a, st = 2, 4

            def step(b, s):
                o = 1 - s
                if exists(b):
                    act.wait_ge(S["rel_done"], b + 1)
                    wait(act, S["r_done"], 4 * b)
                    act.copy(by_head(sT[:, :]), ps[:, 0:4, :].rearrange("p g (b a h) -> p (g b) a h", a=8, h=H))\
                       .then_inc(S["sT_ready"], 1)
                if exists(b - 1):
                    act.wait_ge(S["o_done"], N2(b))
                    wait(act, S["h_turned"], N2(b) - 1)
                    act.copy(headT[:, :], ps[:, 7, :]).then_inc(S["hT_ready"], 1)
                if exists(b + 1):
                    act.wait_ge(S["xT_done"], NB * st + b + 2)
                    wait(act, S["v_done"], N2(b))
                    act.copy(xcT[:, o, :, :], ps[:, 4, :].rearrange("p (k n) -> p k n", k=2 * KT))\
                       .then_inc(S["xT_ready"], 1)
                    act.wait_ge(S["qk_done"], N2(b) + 2)
                    wait(act, q_stored, 16 * (b - 1) + 16)
                    wait(act, S["qd_ready"], 2 * b)
                    wait(act, S["rel_done"], b)
                    for j, (t_, bias, off, n) in enumerate(((qu, bias_q[2], 0, "qu_ready"), (kT, bias_k[2], D, "k_ready"))):
                        for t in range(KT):
                            ins = act.activation(t_[:, o, t, :], ps[:, 5, off + t * P:off + (t + 1) * P], ACT.Identity,
                                                 bias=bias[:, t:t + 1])
                        ins.then_inc(S[n], 1)
                if exists(b):
                    act.wait_ge(S["oh_done"], b + 1)
                    wait(act, S["ov_done"], 4 * b - 4)
                    act.activation(by_head(probs[:, s, :]),
                                   ps[:, 0:4, :].rearrange("p g (b a h) -> p (g b) a h", a=8, h=H), ACT.Exp, scale=SCALE)\
                       .then_inc(S["p_ready"], 1)
                if exists(b + 1):
                    act.wait_ge(z_loaded, 128 * b + 256)
                    for r in range(4, 8):
                        ins = act.mul(q2[:, :, r, :], qz[:, :, :].rearrange("p h b -> p b h"), block8[:, r:r + 1])
                    ins.then_inc(S["q2_high_ready"], 1)
            over_samples(act, step)

        def expand_for_keys(eng, s, t):
            eng.tensor_tensor(qd[:, :, :, t * 8:(t + 1) * 8],
                              bc(qu[:, s, t, :].rearrange("p (a b) -> p b a", b=HD), 8, 3),
                              bc(bc(block8[:, :], 8, 1), HD, 1), ALU.mult).then_inc(S["qd_ready"], 1)

        def expand_queries(pool, m, s):
            pool.wait_ge(S["qu_ready"], m + 1)
            wait(pool, S["rel_done"], m)
            expand_for_keys(pool, s, 0)
            pool.wait_ge(z_loaded, 128 * m + 128)
            for r in range(4):
                ins = pool.tensor_tensor(q2[:, :, r, :], qz[:, :, :].rearrange("p h b -> p b h"),
                                         bc(bc(block8[:, r:r + 1], H, 1).squeeze(2), HD, 1), ALU.mult)
            ins.then_inc(S["q2_ready"], 1)

        def shifted_dve(dve):
            a, st = 2, 4

            def mask_offsets(b):
                for c in range(4):
                    dve.wait_ge(S["ov_done"], 4 * b + c + 1)
                    if c == 0:
                        wait(dve, S["ov_summed"], b)
                    dve.tensor_tensor(by_head(spread_v[:, :])[:, 4 * c:4 * c + 4, :, :],
                                      ps[:, 5 + c % 2, :].rearrange("p (b a h) -> p b a h", a=8, h=H),
                                      bc(bc(block8r[:, :], H, 2), 4, 1), ALU.mult).then_inc(S["ov_masked"], 1)

            def normalise(b, s):
                dve.wait_ge(S["ov_summed"], b + 1)
                dve.tensor_copy(ovT[:, :], ps[:, 4, D:2 * D]).then_inc(S["ov_copied"], 1)
                dve.wait_ge(S["ov_turned"], b + 1)
                dve.wait_ge(S["h_turned"], N2(b) + 1)
                heads = ps[:, 7, :].rearrange("p (h d) -> p h d", d=VW)[:, :, 0:HD + 1]
                dve.reciprocal(rec[:, s, :], heads[:, :, HD]).then_inc(S["rec_ready"], 1)
                dve.wait_ge(S["rec_ready"], N2(b) + 1)
                byh = mix2[:, :].rearrange("p (h d) -> p h d", d=HD)
                dve.tensor_tensor(byh, heads[:, :, 0:HD], bc(rec[:, s, :], HD, 2), ALU.mult)
                dve.tensor_tensor(mix3[:, :].rearrange("p (h d) -> p h d", d=HD),
                                  ps[:, 4, 0:D].rearrange("p (h d) -> p h d", d=HD), bc(rec[:, s, :], HD, 2), ALU.mult)\
                   .then_inc(S["mix2_ready"], 1)
                dve.wait_ge(S["mix2_ready"], b + 1)
                wait(dve, S["oT_done"], N2(b) - 1)
                dve.tensor_tensor(on[:, s, :], mix2[:, :], mix3[:, :], ALU.add).then_inc(S["on_ready"], 1)

            def step(b, s):
                o = 1 - s
                if exists(b):
                    for c in range(4):
                        dve.wait_ge(S["r_done"], 4 * b + c + 1)
                        dve.tensor_reduce(nm[:, s, 4 * c:4 * c + 4], ps[:, 5 + c % 2, :].rearrange("p (j n) -> p j n", n=P),
                                          AX.X, ALU.max, negate=True).then_inc(S["r_read"], 1)
                    dve.wait_ge(S["r_read"], 4 * b + 4)
                    wait(dve, row_loaded, 32 * b)
                    dve.tensor_copy(nm_hl[:, 0, 0, :], nm[:, s, :]).then_inc(S["hi_ready"], 1)
                    dve.wait_ge(S["hi_ready"], b + 1)
                    dve.tensor_tensor(nm_hl[:, 0, 1, :], nm[:, s, :], nm_hl[:, 0, 0, :], ALU.subtract)\
                       .then_inc(S["nm_hl_ready"], 1)
                if exists(b + 1):
                    dve.wait_ge(S["v_done"], N2(b) + 2)
                    wait(dve, S["o_done"], N2(b))
                    dve.tensor_copy(v1[:, o, :, 0:HD], ps[:, 6, 0:D].rearrange("p (h d) -> p h d", d=HD))\
                       .then_inc(S["v_ready"], 1)
                if exists(b - 1):
                    mask_offsets(b - 1)
                if exists(b + 1):
                    dve.wait_ge(S["qu_ready"], b + 2)
                    wait(dve, S["rel_done"], b + 1)
                    expand_for_keys(dve, o, 1)
                if exists(b - 1):
                    normalise(b - 1, o)
                    dve.wait_ge(S["oT_done"], N2(b))
                    wait(dve, S["y_done"], N2(b) - 2)
                    dve.tensor_copy(oT[:, o, :, :], ps[:, 6, 0:D].rearrange("p (k n) -> p k n", k=KT))\
                       .then_inc(S["oT_ready"], 1)
                    dve.wait_ge(S["y_done"], N2(b))
                    wait_bias(dve, st, b - 1)
                    dve.scalar_tensor_tensor(xs(b - 1), ps[:, 4, 0:D], gate(st), xs(b - 1), ALU.mult, ALU.add)\
                       .then_inc(S["x_added"], 1)
                if exists(b + 2) and not (isinstance(b, int) and b < 0):
                    ln_apply(dve, st, b + 2, s, xn[:, s, :])
                if exists(b + 3) and not (isinstance(b, int) and b < 0):
                    ln_stats(dve, st, b + 3, o)
            for m in (0, 1):
                ln_stats(dve, st, m, m)
                ln_apply(dve, st, m, m, xn[:, m, :])
            ln_stats(dve, st, 2, 0)
            over_samples(dve, step)

        def shifted_pool(pool):
            def step(b, s):
                if exists(b + 1):
                    expand_queries(pool, b + 1, 1 - s)
                if exists(b + 3) and not (isinstance(b, int) and b < 0):
                    ln_rstd(pool, 4, b + 3, 1 - s)
                if exists(b + 2) and not (isinstance(b, int) and b < 0):
                    add_bias(pool, 4, b + 2)
            for m in (0, 1):
                ln_rstd(pool, 4, m, m)
                add_bias(pool, 4, m)
            ln_rstd(pool, 4, 2, 0)
            over_samples(pool, step)

        def stage_pool(pool, st):
            if st == 4:
                shifted_pool(pool)
                return
            ln_rstd(pool, st, 0, 0)
            with pool.Fori(1, NB - 2, 2) as m:
                ln_rstd(pool, st, m, 1)
                add_bias(pool, st, m - 1)
                ln_rstd(pool, st, m + 1, 0)
                add_bias(pool, st, m)
            ln_rstd(pool, st, NB - 1, 1)
            add_bias(pool, st, NB - 2)
            add_bias(pool, st, NB - 1)

        def store_out(sp):
            for m in range(0, NB, 8):
                sp.wait_ge(S["x_added"], NB * (STAGES - 1) + m + 8)
                sp.dma_start(out[m:m + 8].rearrange("b p d -> p b d"), x_all[:, m:m + 8, :]).then_inc(out_stored, 16)
            sp.wait_ge(out_stored, 16 * (NB // 8))


        def plain_pe(pe, st):
            half = NB * (st // 4)

            def transpose_in(m, s):
                if st == 1:
                    pe.wait_ge(S["quant_step"], 3 * m + 3)
                else:
                    pe.wait_ge(S["xn_ready"], NB * st + m + 1)
                wait(pe, S["fxT_ready"], half + m - 1)
                for k in range(KT):
                    src = (fq[:, s, 2, :] if st == 1 else fx[:, s, :])[:, k * P:(k + 1) * P]
                    last = pe.transpose(ps[:, s, k * P:(k + 1) * P], src, ident[:, :])
                last.then_inc(S["xT_done"], 1)

            def product(b, s):
                pe.wait_ge(S["fxT_ready"], half + b + 1)
                wait(pe, S["x_added"], NB * st + b - 1)
                if st == 5:
                    wait(pe, S["zw_ready"], b - 1)
                    for k in range(KT):
                        last = pe.matmul(ps[:, 2 + s, 0:G2 + P], fxT[:, s, k, :], gateloraT[:, k, :], start=(k == 0),
                                         stop=(k == KT - 1))
                    last.then_inc(S["route_in"], 1)
                w = ternT if st == 1 else baseT
                for k in range(KT):
                    last = pe.matmul(ps[:, 4 + s, 0:D], fxT[:, s, k, :], w[:, k, :], start=(k == 0),
                                     stop=(k == KT - 1))
                last.then_inc(S["fy_done"], 1)

            def low_rank(b, s):
                pe.wait_ge(S["zw_ready"], b + 1)
                wait(pe, S["zT_ready"], b)
                pe.transpose(ps[:, 6, 0:P], fz[:, s, :], ident[:, :]).then_inc(S["zT_done"], 1)
                pe.wait_ge(S["zT_ready"], b + 1)
                pe.matmul(ps[:, 4 + s, 0:D], fzT[:, s, :], lora_bT[:, :], start=False, stop=True,
                          skip_group_check=True).then_inc(S["f2_done"], 1)

            def step(b, s):
                if exists(b + 1):
                    transpose_in(b + 1, 1 - s)
                if exists(b):
                    product(b, s)
                if st == 5 and exists(b - 1):
                    low_rank(b - 1, 1 - s)
            over_samples(pe, step)

        def plain_act(act, st):
            half = NB * (st // 4)

            def step(b, s):
                o = 1 - s
                if exists(b + 1):
                    act.wait_ge(S["xT_done"], NB * st + b + 2)
                    wait(act, S["fy_done"], half + b)
                    act.copy(fxT[:, o, :, :], ps[:, o, 0:D].rearrange("p (k n) -> p k n", k=KT))\
                       .then_inc(S["fxT_ready"], 1)
                if st == 5 and exists(b):
                    act.wait_ge(S["route_nm"], b + 1)
                    act.activation(f_e[:, s, :], ps[:, 2 + s, 0:G2], ACT.Exp, bias=f_r[:, s, 0:1]).then_inc(S["route_e"], 1)
                if st == 5 and exists(b - 1):
                    act.wait_ge(S["zT_done"], b)
                    act.copy(fzT[:, o, :], ps[:, 6, 0:P]).then_inc(S["zT_ready"], 1)
            over_samples(act, step)

        def plain_dve(dve, st):
            def quantise(m, s):
                dve.wait_ge(S["xn_ready"], NB * st + m + 1)
                wait(dve, S["xT_done"], NB * st + m - 1)
                for i, (src, x1, x2, op0, op1) in enumerate((
                        (fx[:, s, :], act_s[:, 1:2], QB, ALU.mult, ALU.min),
                        (fq[:, s, 0, :], -QB, ROUND, ALU.max, ALU.add),
                        (fq[:, s, 1, :], -ROUND, 0.0, ALU.add, ALU.add))):
                    if i:
                        dve.wait_ge(S["quant_step"], 3 * m + i)
                    dve.tensor_scalar(fq[:, s, i, :], src, x1, x2, op0, op1).then_inc(S["quant_step"], 1)

            def route(b, s):
                STEPS = 9
                at = [0]

                def then(ins):
                    at[0] += 1
                    ins.then_inc(S["route_step"], 1)
                    dve.wait_ge(S["route_step"], STEPS * b + at[0])
                dve.wait_ge(S["route_e"], b + 1)
                dve.memset(tick[:, 1:2], 0.0)
                then(dve.max(f_top[:, s, :], f_e[:, s, :]))
                dve.memset(tick[:, 2:3], 0.0)
                then(dve.max_index(f_ix[:, s, :], f_top[:, s, :], f_e[:, s, :]))
                then(dve.tensor_copy(f_ixf[:, s, 0:2], f_ix[:, s, 0:2]))
                for i in range(2):
                    ins = dve.tensor_scalar(f_s[:, s, i, :], iota10[:, :], f_ixf[:, s, i:i + 1], f_top[:, s, i:i + 1],
                                            ALU.is_equal, ALU.mult)
                then(ins)
                then(dve.tensor_tensor(f_w[:, s, :], f_s[:, s, 0, :], f_s[:, s, 1, :], ALU.add))
                then(dve.tensor_reduce(f_r[:, s, 1:2], f_w[:, s, 0:E2], AX.X, ALU.add))
                then(dve.scalar_tensor_tensor(f_r[:, s, 2:3], f_r[:, s, 1:2], 0.0, f_r[:, s, 1:2], ALU.is_equal, ALU.add))
                then(dve.reciprocal(f_r[:, s, 3:4], f_r[:, s, 2:3]))
                then(dve.tensor_scalar(f_w[:, s, :], f_w[:, s, :], f_r[:, s, 3:4], None, ALU.mult))
                assert at[0] == STEPS
                wait(dve, S["zT_done"], b - 1)
                dve.tensor_tensor(fz[:, s, :].rearrange("p (e r) -> p e r", r=R),
                                  ps[:, 2 + s, G2:G2 + P].rearrange("p (e r) -> p e r", r=R),
                                  bc(f_w[:, s, 0:E2], R, 2), ALU.mult).then_inc(S["zw_ready"], 1)

            def add(b, s):
                if st == 1:
                    dve.wait_ge(S["fy_done"], b + 1)
                else:
                    dve.wait_ge(S["f2_done"], b + 1)
                wait_bias(dve, st, b)
                dve.scalar_tensor_tensor(xs(b), ps[:, 4 + s, 0:D], act_s[:, 2:3] if st == 1 else gate(st), xs(b),
                                         ALU.mult, ALU.add).then_inc(S["x_added"], 1)

            def step(b, s):
                o = 1 - s
                if st == 5 and exists(b):
                    dve.wait_ge(S["route_in"], b + 1)
                    dve.tensor_reduce(f_r[:, s, 0:1], ps[:, 2 + s, 0:G2], AX.X, ALU.max, negate=True)\
                       .then_inc(S["route_nm"], 1)
                if exists(b + 2) and not (isinstance(b, int) and b < 0):
                    ln_apply(dve, st, b + 2, s, fx[:, s, :])
                    if st == 1:
                        quantise(b + 2, s)
                if exists(b + 3) and not (isinstance(b, int) and b < 0):
                    ln_stats(dve, st, b + 3, o)
                if st == 1 and exists(b):
                    add(b, s)
                if st == 5:
                    if exists(b):
                        route(b, s)
                    if exists(b - 1):
                        add(b - 1, o)
            for m in (0, 1):
                ln_stats(dve, st, m, m)
                ln_apply(dve, st, m, m, fx[:, m, :])
                if st == 1:
                    quantise(m, m)
            ln_stats(dve, st, 2, 0)
            over_samples(dve, step)

        def over_groups(eng, step):
            for g in range(-1, 3):
                step(g, g % 2)
            with eng.Fori(3, NG - 4, 2) as g:
                step(g, 1)
                step(g + 1, 0)
            for g in range(NG - 3, NG + 1):
                step(g, g % 2)

        def group_exists(g):
            return not isinstance(g, int) or 0 <= g < NG

        def group_norm(dve, st, g, s):
            for half in range(GROUP // 2):
                for i in range(2):
                    ln_stats(dve, st, GROUP * g + 2 * half + i, i)
                for i in range(2):
                    j = 2 * half + i
                    ln_apply(dve, st, GROUP * g + j, i, (gx3 if st == 7 else gx)[:, s, j, :], slots=2 * GROUP)

        def group_transpose(pe, st, g, s):
            done = NG * (st // 4)
            pe.wait_ge(S["xn_ready"], NB * st + GROUP * (g + 1))
            wait(pe, S["gxT_ready"], 2 * (done + g))
            for j in range(GROUP):
                for k in range(KT):
                    last = pe.transpose(ps[:, 4 + k, j * P:(j + 1) * P],
                                        (gx3 if st == 7 else gx)[:, s, j, k * P:(k + 1) * P], ident[:, :])
                last.then_inc(S["xT_done"], 1)

        def group_copy(act, st, g, s, free, value):
            act.wait_ge(S["xT_done"], NB * st + GROUP * (g + 1))
            wait(act, free, value)
            for k in range(KT):
                act.copy((gxT3 if st == 7 else gxT)[:, s, k, :], ps[:, 4 + k, :]).then_inc(S["gxT_ready"], 1)

        def wide_pe(pe):
            st = 3

            def hidden(g, s):
                pe.wait_ge(S["gxT_ready"], 2 * g + 2)
                for f in range(FT):
                    wait(pe, S["hid_ready"], FT * g + f - 3)
                    for k in range(KT):
                        last = pe.matmul(ps[:, f % 4, :], fcT[:, k, f * P:(f + 1) * P], gxT[:, s, k, :], start=(k == 0),
                                         stop=(k == KT - 1))
                    last.then_inc(S["hid_done"], 1)

            def product(g, s):
                pe.wait_ge(S["hid_ready"], FT * (g + 1))
                for j in range(GROUP):
                    wait(pe, S["x_added"], NB * st + GROUP * g + j - 1)
                    for f in range(FT):
                        last = pe.matmul(ps[:, 6 + j % 2, 0:D], hid[:, f, j * P:(j + 1) * P], projT[:, f, :],
                                         start=(f == 0), stop=(f == FT - 1))
                    last.then_inc(S["wide_done"], 1)

            def step(g, s):
                if group_exists(g):
                    hidden(g, s)
                if group_exists(g + 1):
                    group_transpose(pe, st, g + 1, 1 - s)
                if group_exists(g):
                    product(g, s)
            over_groups(pe, step)

        def wide_act(act):
            def step(g, s):
                if group_exists(g):
                    for f in range(FT):
                        act.wait_ge(S["hid_done"], FT * g + f + 1)
                        wait(act, S["wide_done"], GROUP * g)
                        act.activation(hid[:, f, :], ps[:, f % 4, :], ACT.Gelu, bias=b_fc[:, f:f + 1])\
                           .then_inc(S["hid_ready"], 1)
                if group_exists(g + 1):
                    group_copy(act, 3, g + 1, 1 - s, S["hid_done"], FT * g)
            over_groups(act, step)

        def wide_dve(dve):
            st = 3

            def step(g, s):
                if group_exists(g + 2) and not (isinstance(g, int) and g < 0):
                    group_norm(dve, st, g + 2, s)
                if group_exists(g):
                    for j in range(GROUP):
                        m = GROUP * g + j
                        dve.wait_ge(S["wide_done"], m + 1)
                        wait_bias(dve, st, m)
                        dve.scalar_tensor_tensor(xs(m), ps[:, 6 + j % 2, 0:D], gate(st), xs(m), ALU.mult, ALU.add)\
                           .then_inc(S["x_added"], 1)
            group_norm(dve, st, 0, 0)
            group_norm(dve, st, 1, 1)
            over_groups(dve, step)

        def choose_pe(pe):
            st = 7

            def logits(g, s):
                pe.wait_ge(S["gxT_ready"], 2 * (NG + g) + 2)
                wait(pe, S["lg_ready"], g)
                for j in range(GROUP):
                    for k in range(KT):
                        last = pe.matmul(ps[NE * j:NE * (j + 1), 0, 0:P], gate3T[:, k, :],
                                         gxT3[:, s, k, j * P:(j + 1) * P], start=(k == 0), stop=(k == KT - 1))
                last.then_inc(S["lg_done"], 1)

            def merge(g, s):
                pe.wait_ge(S["mk_ready"], g + 1)
                wait(pe, S["mT_ready"], g)
                pe.transpose(ps[:, 1, 0:P], mk[:, s, :], ident[:, :]).then_inc(S["mT_done"], 1)
                pe.wait_ge(S["mT_ready"], g + 1)
                wait(pe, S["mg_ready"], g)
                for t in range(KT):
                    for j in range(GROUP):
                        last = pe.matmul(ps[:, 2, t * P + NE * j:t * P + NE * (j + 1)], gx3[:, s, j, t * P:(t + 1) * P],
                                         mT[:, s, NE * j:NE * (j + 1)], start=True, stop=True)
                last.then_inc(S["mg_done"], 1)

            def step(g, s):
                if group_exists(g):
                    logits(g, s)
                if group_exists(g - 1):
                    merge(g - 1, 1 - s)
                if group_exists(g + 1):
                    group_transpose(pe, st, g + 1, 1 - s)
            over_groups(pe, step)

        def choose_act(act):
            def step(g, s):
                if group_exists(g):
                    act.wait_ge(S["lg_done"], g + 1)
                    wait(act, S["l3_e"], g - 1)
                    act.activation(lg[:, s, :], ps[:, 0, 0:P], ACT.Identity, bias=gate_b4[:, :]).then_inc(S["lg_ready"], 1)
                if group_exists(g - 1):
                    act.wait_ge(S["mT_done"], g)
                    wait(act, S["mg_done"], g - 2)
                    act.copy(mT[:, 1 - s, :], ps[:, 1, 0:P]).then_inc(S["mT_ready"], 1)
                    act.wait_ge(S["mg_done"], g)
                    for t in range(KT):
                        src = ps[:, 2, t * P:(t + 1) * P].rearrange("p (j e) -> p e j", j=GROUP)
                        m = GROUP * (g - 1)
                        ins = act.copy(merged[:, t, :, m:m + GROUP] if isinstance(m, int) else
                                       merged[:, t, :, bass.ds(m, GROUP)], src)
                    ins.then_inc(S["mg_ready"], 1)
                if group_exists(g):
                    act.wait_ge(S["l3_step"], 6 * g + 1)
                    act.activation(pe_[:, s, :], lg[:, s, :], ACT.Exp, bias=sm[:, 0:1], accum_out=sm[:, 1:2])\
                       .then_inc(S["l3_e"], 1)
                if group_exists(g + 1):
                    group_copy(act, 7, g + 1, 1 - s, S["lg_done"], g)
            over_groups(act, step)

        def choose_dve(dve):
            def choose(g, s):
                STEPS = 6
                at = [0]

                def then(ins):
                    at[0] += 1
                    ins.then_inc(S["l3_step"], 1)
                    dve.wait_ge(S["l3_step"], STEPS * g + at[0])
                dve.wait_ge(S["lg_ready"], g + 1)
                wait(dve, S["l3_e"], g)
                then(dve.tensor_reduce(sm[:, 0:1], lg[:, s, :], AX.X, ALU.max, negate=True))
                dve.wait_ge(S["l3_e"], g + 1)
                then(dve.reciprocal(sm[:, 2:3], sm[:, 1:2]))
                then(dve.tensor_scalar(pe_[:, s, :], pe_[:, s, :], sm[:, 2:3], None, ALU.mult))
                dve.memset(tick[:, 1:2], 0.0)
                then(dve.max(top[:, :], pe_[:, s, :]))
                dve.memset(tick[:, 2:3], 0.0)
                then(dve.match_replace(rep[:, :], top[:, :], pe_[:, s, :], -1.0))
                wait(dve, S["mT_done"], g - 1)
                wait(dve, route_stored, 16 * g)
                then(dve.scalar_tensor_tensor(mk[:, s, :], rep[:, :], 0.0, pe_[:, s, :], ALU.is_lt, ALU.mult))
                dve.wait_ge(S["l3_step"], STEPS * g + 6)
                dve.memset(sm[:, 3:4], 0.0).then_inc(S["mk_ready"], 1)

            def step(g, s):
                if group_exists(g + 1) and not (isinstance(g, int) and g < 0):
                    wait(dve, S["mg_done"], g)
                    group_norm(dve, 7, g + 1, 1 - s)
                if group_exists(g):
                    choose(g, s)
            group_norm(dve, 7, 0, 0)
            over_groups(dve, step)

        def choose_sp(sp):
            sp.wait_ge(S["x_added"], NB * 7)
            for e in range(2):
                load_w1(sp, e, e)
                load_w2(sp, e, e)

            def store(g, s):
                sp.wait_ge(S["mk_ready"], g + 1)
                sp.dma_start(route[g] if isinstance(g, int) else route[bass.ds(g, 1)].squeeze(0), mk[:, s, :])\
                  .then_inc(route_stored, 16)

            def step(g, s):
                if group_exists(g):
                    store(g, s)
            over_groups(sp, step)

        def of_expert(ap, e):
            return ap[e] if isinstance(e, int) else ap[bass.ds(e, 1)].squeeze(0)

        def load_w1(sp, e, s):
            w1 = of_expert(A["L3_ffn_w1"], e)
            sp.dma_start(w1s[s], w1[0:D, :].rearrange("(k p) n -> p k n", p=P)).then_inc(w1_loaded[s], 16)
            sp.dma_start(w1b[:, s, :], w1[D:D + 1, :]).then_inc(w1_loaded[s], 16)

        def load_w2(sp, e, s):
            w2 = of_expert(A["L3_ffn_w2"], e)
            sp.dma_start(w2s[:, s, :, :], w2[0:FE, :].rearrange("(c p) n -> p c n", p=P)).then_inc(w2_loaded[s], 16)
            sp.dma_start(w2b[:, s, :], w2[FE:FE + 1, :]).then_inc(w2_loaded[s], 16)

        def over_experts(eng, step):
            for e in (-1, 0):
                step(e, e % 2)
            with eng.Fori(1, NE - 4, 2) as e:
                step(e, 1)
                step(e + 1, 0)
            for e in range(NE - 3, NE + 1):
                step(e, e % 2)

        def expert_exists(e):
            return not isinstance(e, int) or 0 <= e < NE

        def experts_sp(sp):
            def step(e, s):
                if expert_exists(e) and expert_exists(e + 2):
                    sp.wait_ge(S["h_done"], e + 1)
                    load_w1(sp, e + 2, s)
                if expert_exists(e - 1) and expert_exists(e + 1):
                    sp.wait_ge(S["e_done"], e)
                    load_w2(sp, e + 1, 1 - s)
                if expert_exists(e - 1):
                    sp.wait_ge(S["e_ready"], e)
                    dst = expert_out[:, e - 1, :] if isinstance(e, int) else expert_out[:, bass.ds(e - 1, 1), :].squeeze(1)
                    sp.dma_start(dst, o3[:, 1 - s, :]).then_inc(o_stored[1 - s], 16)
            over_experts(sp, step)
            for i in range(2):
                sp.wait_ge(o_stored[i], 16 * NE // 2)
            sp.wait_ge(route_stored, 16 * NG)
            for g in range(NG):
                i = g % 2
                wait(sp, S["fin_done"], g - 1)
                sp.dma_start(m4[:, i, :], route[g]).then_inc(mo_loaded[i], 16)
                sp.dma_start(o4[:, i, :], expert_out[GROUP * g:GROUP * (g + 1)].rearrange("b e d -> (b e) d"))\
                  .then_inc(mo_loaded[i], 16)

        def experts_pe(pe):
            def up(e, s):
                pe.wait_ge(w1_loaded[s], 32 + 16 * (e - s))
                if isinstance(e, int) and e == 0:
                    pe.wait_ge(S["mg_ready"], NG)
                wait(pe, S["h_ready"], e - 1)
                for c in range(CE):
                    cols = slice(c * P, (c + 1) * P)
                    for k in range(KT):
                        rhs = merged[:, k, e, :] if isinstance(e, int) else merged[:, k, bass.ds(e, 1), :].squeeze(1)
                        pe.matmul(ps[:, s, c * NB:(c + 1) * NB], w1s[s][:, k, cols], rhs, start=(k == 0), stop=False)
                    last = pe.matmul(ps[:, s, c * NB:(c + 1) * NB], w1b[0:1, s, cols], ones[0:1, 0:NB], start=False,
                                     stop=True)
                last.then_inc(S["h_done"], 1)

            def down(e, s):
                pe.wait_ge(w2_loaded[s], 32 + 16 * (e - s))
                pe.wait_ge(S["h_ready"], e + 1)
                wait(pe, S["e_ready"], e - 1)
                for c in range(CE):
                    pe.matmul(ps[0:NB, 2 + s, 0:D], h3[s][:, c * NB:(c + 1) * NB], w2s[:, s, c, :], start=(c == 0),
                              stop=False)
                pe.matmul(ps[0:NB, 2 + s, 0:D], ones[0:1, 0:NB], w2b[0:1, s, :], start=False, stop=True)\
                  .then_inc(S["e_done"], 1)

            def step(e, s):
                if expert_exists(e + 1):
                    up(e + 1, 1 - s)
                if expert_exists(e):
                    down(e, s)
            over_experts(pe, step)
            for g in range(NG):
                pe.wait_ge(mo_loaded[g % 2], 32 * (g // 2 + 1))
                if g == 0:
                    pe.wait_ge(S["e_ready"], NE)
                wait(pe, S["x_added"], NB * 7 + GROUP * (g - 1))
                for j in range(GROUP):
                    rows = slice(NE * j, NE * (j + 1))
                    last = pe.matmul(ps[:, 4 * (g % 2) + j, 0:D], m4[rows, g % 2, :], o4[rows, g % 2, :], start=True,
                                     stop=True)
                last.then_inc(S["fin_done"], 1)

        def experts_act(act):
            def step(e, s):
                if expert_exists(e + 1):
                    act.wait_ge(S["h_done"], e + 2)
                    wait(act, S["e_done"], e)
                    act.activation(h3[1 - s][:, 0:CE * NB], ps[:, 1 - s, 0:CE * NB], ACT.Gelu).then_inc(S["h_ready"], 1)
            over_experts(act, step)

        def experts_dve(dve):
            def step(e, s):
                if expert_exists(e):
                    dve.wait_ge(S["e_done"], e + 1)
                    if not (isinstance(e, int) and e < 2):
                        dve.wait_ge(o_stored[s], 8 * (e - s))
                    dve.tensor_copy(o3[:, s, :], ps[0:NB, 2 + s, 0:D]).then_inc(S["e_ready"], 1)
            over_experts(dve, step)
            for g in range(NG):
                dve.wait_ge(S["fin_done"], g + 1)
                i = 4 * (g % 2)
                dve.scalar_tensor_tensor(x_all[:, GROUP * g:GROUP * (g + 1), :], ps[:, i:i + GROUP, 0:D], gate(7),
                                         x_all[:, GROUP * g:GROUP * (g + 1), :], ALU.mult, ALU.add)\
                   .then_inc(S["x_added"], GROUP)

        def stage(st, name, eng):
            if st == 4:
                {"sp": shifted_sp, "pe": shifted_pe, "act": shifted_act, "dve": shifted_dve}[name](eng)
            elif st in (1, 5) and name != "sp":
                {"pe": plain_pe, "act": plain_act, "dve": plain_dve}[name](eng, st)
            elif st == 3 and name != "sp":
                {"pe": wide_pe, "act": wide_act, "dve": wide_dve}[name](eng)
            elif st == 7:
                {"sp": choose_sp, "pe": choose_pe, "act": choose_act, "dve": choose_dve}[name](eng)
                {"sp": experts_sp, "pe": experts_pe, "act": experts_act, "dve": experts_dve}[name](eng)
            elif st % 2 == 0:
                {"sp": attention_sp, "pe": attention_pe, "act": attention_act, "dve": attention_dve}[name](eng, st // 2)

        block = ctx.enter_context(nc.Block())

        @block.vector
        def _(dve):
            setup_dve(dve)
            for st in range(STAGES):
                stage(st, "dve", dve)

        @block.sync
        def _(sp):
            setup_loads(sp)
            for st in range(STAGES):
                stage(st, "sp", sp)
            store_out(sp)

        @block.gpsimd
        def _(pool):
            setup_pool(pool)
            for st in range(STAGES):
                stage_pool(pool, st)

        @block.scalar
        def _(act):
            setup_act(act)
            for st in range(STAGES):
                stage(st, "act", act)

        @block.tensor
        def _(pe):
            setup_pe(pe)
            for st in range(STAGES):
                stage(st, "pe", pe)


def kernel(**inputs):
    import numpy as _np
    import concourse.bacc as _bacc
    from concourse import mybir as _mybir
    from concourse.bass_utils import run_bass_kernel_spmd as _run

    nc = _bacc.Bacc("TRN2", target_bir_lowering=False, num_devices=1)
    arrays, tensors = {}, {}
    for name, value in inputs.items():
        a = _np.ascontiguousarray(value)
        if a.ndim == 0:
            a = a.reshape(1)
        arrays[f"in_{name}"] = a
        tensors[name] = nc.dram_tensor(f"in_{name}", a.shape, _mybir.dt.from_np(a.dtype), kind="ExternalInput").ap()
    out = nc.dram_tensor("out_0", inputs["x"].shape, _mybir.dt.float32, kind="ExternalOutput").ap()
    flamingo_program(nc, tensors, out)
    r = _run(nc, [arrays], core_ids=[0])
    return r.results[0]["out_0"]
```
